# Optimizing a Trainium2 kernel written in Bass

```python
import numpy as np
import jax
import jax.numpy as jnp

def _softmax(x, axis=-1):
    return jax.nn.softmax(x, axis=axis)
def _gelu(x):
    return jax.nn.gelu(x, approximate=True)
def _silu(x):
    return jax.nn.silu(x)
def _sigmoid(x):
    return jax.nn.sigmoid(x)
def _layernorm(x, axis=-1, eps=1e-5):
    m = jnp.mean(x, axis=axis, keepdims=True)
    v = jnp.var(x, axis=axis, keepdims=True)
    return (x - m) / jnp.sqrt(v + eps)
def _scatter_add(tgt, idx, src, axis=0):
    return tgt.at[idx].add(src)
def _segment_sum(src, seg, n):
    return jax.ops.segment_sum(src, seg, n)

kernel_name = 'mk_adj_preln_d1_adj_64_45dae1'

def setup_inputs(seed: int = 0):
    np.random.seed(seed)
    _w = jnp.asarray
    def _rec_inputs():
        import jax
        import jax.numpy as jnp
        _gk = jax.random.key(seed)
        x = -9.806e-05 + 1 * jax.random.normal(jax.random.fold_in(_gk, 1), (8192, 64), jnp.float32)
        _w = (1.0 + jnp.arange(8192, dtype=jnp.float32)) ** -0.5
        _w = _w / _w.mean()
        _pij = jnp.clip(0.000488281 * _w[:, None] * _w[None, :], 0.0, 1.0)
        _a = jax.random.uniform(jax.random.fold_in(_gk, 2), (8192, 8192)) < _pij
        adj = _a.astype(jnp.int32)
        return x, adj
    x, adj = _rec_inputs()
    def _L0_gnn_setup():
        import jax, jax.numpy as jnp
        import numpy as np
        ALPHA = 0.2
        NEG_BIG = jnp.float32(-9000000000000000.0)
        key = jax.random.key(seed)
        k1, k2, k3, k4 = jax.random.split(key, 4)
        N, F_IN, F_OUT = (8192, 64, 64)
        inputs = jax.random.normal(k1, (N, F_IN), dtype=jnp.float32)
        adj = jax.random.randint(k2, (N, N), 0, 2, dtype=jnp.int32)
        gain = 1.414
        lim_w = gain * np.sqrt(6.0 / (F_IN + F_OUT))
        W = jax.random.uniform(k3, (F_IN, F_OUT), dtype=jnp.float32, minval=-lim_w, maxval=lim_w)
        lim_a = gain * np.sqrt(6.0 / (2 * F_OUT + 1))
        a = jax.random.uniform(k4, (2 * F_OUT, 1), dtype=jnp.float32, minval=-lim_a, maxval=lim_a)
        return {'inputs': inputs, 'adj': adj, 'W': W, 'a': a}
    _L0_gnn_all = _L0_gnn_setup()
    _L0_gnn_in = {k: v for k, v in _L0_gnn_all.items() if k in ('W', 'a', )}
    del _L0_gnn_all

    return {
        "x": x,
        "adj": adj,
        "L0_gnn_W": _L0_gnn_in["W"],
        "L0_gnn_a": _L0_gnn_in["a"],
    }

def reference(x, adj, L0_gnn_W, L0_gnn_a):
    import jax
    import jax.numpy as jnp
    def _L0_gnn_ref(inputs, adj, W, a):
        import jax, jax.numpy as jnp
        import numpy as np
        ALPHA = 0.2
        NEG_BIG = jnp.float32(-9000000000000000.0)
        Wh = inputs @ W
        F_out = W.shape[1]
        a_src = a[:F_out, 0]
        a_dst = a[F_out:, 0]
        e = (Wh @ a_src)[:, None] + (Wh @ a_dst)[None, :]
        e = jnp.where(e > 0, e, ALPHA * e)
        scores = jnp.where(adj > 0, e, NEG_BIG)
        attention = jax.nn.softmax(scores, axis=1)
        h_prime = attention @ Wh
        return jax.nn.elu(h_prime)

    h = jnp.maximum(_layernorm(x, axis=-1), 0.0)
    x = x + _L0_gnn_ref(h, adj, L0_gnn_W, L0_gnn_a)
    return x


_drawn_inputs = setup_inputs


def setup_inputs(seed=0):
    import zlib

    import numpy as np

    out = dict(_drawn_inputs(seed))
    spreads = {}
    factors = {}
    for name, (base, spread) in spreads.items():
        noise = np.random.default_rng([zlib.crc32(name.encode()), seed]).standard_normal(out[name].shape)
        drawn = base * np.exp(spread * noise) if base else spread * noise
        out[name] = jnp.asarray(drawn.astype(out[name].dtype))
    for name, factor in factors.items():
        out[name] = (out[name] * factor).astype(out[name].dtype)
    return out
```

```python
import concourse.bass as bass
from concourse import mybir
from contextlib import ExitStack


def gat_preln_program(nc, x, adj, w, a, out):
    fp32 = mybir.dt.float32
    fp16 = mybir.dt.float16
    i32 = mybir.dt.int32
    ALU = mybir.AluOpType
    ACT = mybir.ActivationFunctionType
    AX = mybir.AxisListType
    MAX = bass.bass_isa.ReduceOp.max
    ADD = bass.bass_isa.ReduceOp.add

    P = 128
    N, F = x.shape
    T = N // P
    HALVES = P // F
    Q = T // HALVES
    ALPHA = 0.2
    EPS = 1e-5
    SPAN = 8.5
    LO = 2048.0
    VTOP = 32000.0
    DTOP = 16384.0
    OFF = -1.0e38

    IB = 1024
    NB = N // IB
    RT = IB // P
    JC = 512
    JP = 256
    JT = JP // P
    NS = N // JP
    SLOTS = 4
    SPL = JC // JP
    CYC = SLOTS * SPL
    W = JT * IB
    WA = 1376
    WA_END = WA - 512
    DW = 32
    RND = 1 + RT // 2
    LIGHT = (0, *range(2, 2 + RND))
    ITEMS = 2 * 3
    VALUE_STEPS = (1, 4, 7, 10, 14, 17)
    NP = NS // 2

    XG = 4
    XT = T // XG
    XQ = XT // HALVES
    FX = F + 2

    x_t = x.rearrange("(t p) f -> p t f", p=P)
    out_t = out.rearrange("(t p) f -> p t f", p=P)
    adj_t = adj.rearrange("(t p) j -> p t j", p=P)

    sd_dram = nc.dram_tensor("sd_rows", [2, N], fp32, kind="Internal").ap()

    ctx = ExitStack()
    with ctx:
        def sb(name, shape, dt=fp32):
            return ctx.enter_context(nc.sbuf_tensor(name, shape, dt))

        def sem(name):
            return ctx.enter_context(nc.semaphore(name))

        ring = sb("ring", [P, SLOTS * RT * JC], i32)
        slots = ring[:, :].rearrange("p (s t j) -> p s t j", s=SLOTS, t=RT)
        gen_adj = ring[:, 0:N]
        s_rows = sb("s_rows", [P, N])
        d_rows = s_rows
        feat = sb("feat", [P, 2 * T * P], fp16)
        feats = feat[:, :].rearrange("p (k t c) -> p k t c", k=2, t=T)
        gen_p = feat[:, :].bitcast(fp32)
        den_w = sb("den_w", [P, 2, T, 2], fp16)
        den_pad = sb("den_pad", [P, 2, 2, JT, DW], fp16)
        mask = sb("mask", [P, 2, RT, JP], fp16)
        big = sb("big", [P, 13 * 1024])
        hT = big[:, 0:T // HALVES * P]
        xa = feat[:, :].bitcast(fp32)[:, 0:T * F].rearrange("p (t f) -> p t f", t=T)
        sq = feat[:, :].bitcast(fp32)[:, T * F:2 * T * F].rearrange("p (t f) -> p t f", t=T)
        wh0 = 3 * W
        whx = big[:, wh0:wh0 + T * FX].rearrange("p (t c) -> p t c", c=FX)
        wh = whx[:, :, 0:F]
        tail0 = wh0 + T * FX
        fscaled = [big[:, tail0 + n * XT * F:tail0 + (n + 1) * XT * F]
                   .rearrange("p (t f) -> p t f", t=XT) for n in range(2)]
        gen_pT = big[:, tail0:tail0 + 2 * 512]
        gen_x = big[:, tail0 + 1024:tail0 + 1024 + F]
        gen_o = big[:, tail0 + 1088:tail0 + 1088 + F]
        gen_e = big[:, tail0 + 1152:tail0 + 1152 + F]
        big16 = big[:, :].bitcast(fp16)
        code = big16[:, 0:2 * W].rearrange("p (b w) -> p b w", b=2)
        m_pos = big16[:, 2 * W:4 * W].rearrange("p (b w) -> p b w", b=2)
        m_neg = big16[:, 4 * W:6 * W].rearrange("p (b w) -> p b w", b=2)
        fast0 = 3 * W
        acc_sb = big[:, fast0:fast0 + 2 * IB].rearrange("p (k i) -> p k i", k=2)
        den_sb = big[:, fast0 + 2 * IB:fast0 + 2 * IB + 512]
        at = fast0 + 2 * IB + 512
        ends = big[:, at:at + 2048].rearrange("p (t k c) -> p t k c", t=RT, k=2)
        end_lo = ends[:, :, :, F:P]
        at2 = at + 2048
        num = big[:, at2:at2 + 512].rearrange("p (t f) -> p t f", t=RT)
        elu = big[:, at2 + 512:at2 + 1024].rearrange("p (t f) -> p t f", t=RT)
        res = big[:, at2 + 1024:at2 + 1536].rearrange("p (t f) -> p t f", t=RT)

        w2 = sb("w2", [P, FX])
        a2 = sb("a2", [F, 2])
        wT = sb("wT", [F, P])
        ident = sb("ident", [P, P])
        ident16 = sb("ident16", [P, P], fp16)
        ones_n = sb("ones_n", [P, P])
        mean_wh = sb("mean_wh", [P, F])
        stat = sb("stat", [P, 6, T])
        rstd = sb("rstd", [P, T])
        sdT = sb("sdT", [P, P])
        sd = sb("sd", [P, 2, T])
        neg_d = sb("neg_d", [P, T])
        ext = sb("ext", [P, 4])
        allx = sb("allx", [P, 4])
        sc = sb("sc", [P, 12])
        flag = sb("flag", [P, 1], i32)
        e_pos = sb("e_pos", [P, T])
        e_neg = sb("e_neg", [P, T])
        scaled = sb("scaled", [P, 2, T])
        row_f = sb("row_f", [P, T, 2])
        den_end = sb("den_end", [P, 4, 2, 2, 2])
        den_k = sb("den_k", [P, 4, 2, 2])
        den_row = sb("den_row", [P, 2, 4])
        no_edge = sb("no_edge", [P, 2, 4])
        recip = sb("recip", [P, RT])
        g1 = sb("g1", [P, 8])

        minus_half = sc[:, 11:12]
        w_sq = stat[:, 5, 0:F]

        bank = [ctx.enter_context(nc.psum_tensor(f"bank{k}", [P, 512], fp32)) for k in range(8)]
        tr = [bank[k][:, :].bitcast(fp16) for k in (0, 1)]
        acc = [[bank[2], bank[3]], [bank[4], bank[5]]]
        den = bank[6]
        end = bank[7]

        x_in, w_in = [sem(f"x_in{k}") for k in range(XG)], sem("w_in")
        adj_in = [sem(f"adj_in{k}") for k in range(SLOTS)]
        adj_used = sem("adj_used")
        mask_used = sem("mask_used")
        coded = sem("coded")
        neg_act = sem("neg_act")
        masks_dve = sem("masks_dve")
        masks_free = sem("masks_free")
        pad_ready = sem("pad_ready")
        acc_act, acc_dve = sem("acc_act"), sem("acc_dve")
        sums_done = sem("sums_done")
        round_pe = sem("round_pe")
        round_act = sem("round_act")
        ends_free = sem("ends_free")
        den_ready, recip_ready = sem("den_ready"), sem("recip_ready")
        pool_c = sem("pool_c")
        elu_in, elu_out = sem("elu_in"), sem("elu_out")
        res_in, res_done, stored = sem("res_in"), sem("res_done"), sem("stored")
        dve, mean_ready, pool_s = sem("dve"), sem("mean_ready"), sem("pool_s")
        mean_in = sem("mean_in")
        pool_waits = sem("pool_waits")
        num_free, gen_free = sem("num_free"), sem("gen_free")
        consts, centered, sq_done = sem("consts"), sem("centered"), sem("sq_done")
        var_ready, root_done, xT_done, relu_done = (sem("var_ready"), sem("root_done"), sem("xT_done"),
                                                    sem("relu_done"))
        wT_done, wTc, wa_done, wac = sem("wT_done"), sem("wTc"), sem("wa_done"), sem("wac")
        wh_pe, wh_copied = sem("wh_pe"), sem("wh_copied")
        sd_ready, sdT_pe, sdT_ready, sd_out = sem("sd_ready"), sem("sdT_pe"), sem("sdT_ready"), sem("sd_out")
        rows_in, rows_in2 = sem("rows_in"), sem("rows_in2")
        den_w_ready, feat_c = sem("den_w_ready"), sem("feat_c")
        scaled_ready = sem("scaled_ready")
        ext_ready, ext_all, scal, exps = sem("ext_ready"), sem("ext_all"), sem("scal"), sem("exps")
        fsc_ready, fhi_ready, fts = sem("fsc_ready"), sem("fhi_ready"), sem("fts")
        rows_ready, mean_pe, flag_ready = sem("rows_ready"), sem("mean_pe"), sem("flag_ready")
        g_in, g_x, g_rows = sem("g_in"), sem("g_x"), sem("g_rows")
        g_score, g_exp, g_tr, g_trc = sem("g_score"), sem("g_exp"), sem("g_tr"), sem("g_trc")
        g_pv, g_read, g_n, g_e, g_o, g_st = (sem("g_pv"), sem("g_read"), sem("g_n"), sem("g_e"),
                                             sem("g_o"), sem("g_st"))

        def is_fast(eng):
            eng.wait_ge(flag_ready, 1)
            return eng.value_load(flag[0:1, 0:1], min_val=0, max_val=1)

        block = ctx.enter_context(nc.Block())

        @block.sync
        def _(sp):
            sp.dma_start(xa[:, 0:XT, :], x_t[:, 0:XT, :]).then_inc(x_in[0], 16)
            for h in range(HALVES):
                sp.dma_start(w2[h * F:(h + 1) * F, 0:F], w).then_inc(w_in, 16)
            for k in range(2):
                sp.dma_start(a2[:, k:k + 1], a[k * F:(k + 1) * F, :]).then_inc(w_in, 16)
            for g in range(1, XG):
                sp.dma_start(xa[:, bass.ts(g, XT), :], x_t[:, bass.ts(g, XT), :]).then_inc(x_in[g], 16)

            def load(b, c, slot):
                sp.dma_start(slots[:, slot], adj_t[:, bass.ds(b * RT, RT), bass.ds(c * JC, JC)])\
                    .then_inc(adj_in[slot], 16)

            for k in range(SLOTS):
                load(0, k, k)
            sp.wait_ge(sdT_ready, 1)
            sp.dma_start(sd_dram.rearrange("k (t p) -> (k t) p", p=P), sdT[:, :]).then_inc(sd_out, 16)
            sp.wait_ge(sd_out, 16)
            sp.dma_start(s_rows[:, 0:IB], sd_dram[0:1, 0:IB].to_broadcast([P, IB])).then_inc(rows_in, 16)
            sp.dma_start(s_rows[:, IB:N], sd_dram[0:1, IB:N].to_broadcast([P, N - IB]))\
                .then_inc(rows_in2, 16)
            fast = is_fast(sp)
            with sp.If(fast == 1):
                def turn(b, m, used):
                    for k in range(SLOTS):
                        sp.wait_ge(adj_used, used + (k + 1) * SPL)
                        load(b, m * SLOTS + k, k)

                TURNS = NS // CYC
                with sp.Fori(0, TURNS - 1) as m:
                    turn(0, m + 1, m * CYC)
                with sp.Fori(0, NB - 1) as b:
                    with sp.Fori(0, TURNS) as m:
                        turn(b + 1, m, b * NS + m * CYC + (NS - CYC))
            with sp.If(fast == 0):
                for k in range(SLOTS):
                    sp.wait_ge(adj_in[k], 16)
                sp.wait_ge(rows_in, 16)
                sp.wait_ge(rows_in2, 16)
                sp.dma_start(d_rows[:, :], sd_dram[1:2, :].to_broadcast([P, N])).then_inc(g_rows, 16)
                with sp.Fori(0, T) as t:
                    sp.wait_ge(g_score, t + 1)
                    sp.dma_start(gen_adj, adj[bass.ds(t * P, P), :]).then_inc(g_in, 16)
                    sp.wait_ge(g_o, t + 1)
                    sp.dma_start(gen_x, x[bass.ds(t * P, P), :]).then_inc(g_x, 16)

        @block.gpsimd
        def _(pool):
            def held():
                pool.sem_inc(pool_waits, 1)

            nc.gpsimd.memset(ident[:, :], 0.0).then_inc(pool_s, 1)
            nc.gpsimd.memset(ones_n[:, :], 1.0 / N).then_inc(pool_s, 1)
            nc.gpsimd.memset(den_pad[:, :, :, :, :], 0.0).then_inc(pool_s, 1)
            pool.wait_ge(pool_s, 3)

            def put(ap, value, base, pattern):
                return nc.gpsimd.affine_select(out=ap, in_=ap, compare_op=ALU.not_equal, fill=value,
                                               base=base, pattern=pattern, channel_multiplier=1)

            put(ident[:, :], 1.0, 0, [[-1, P]]).then_inc(pool_s, 1)
            pool.wait_ge(pool_s, 4)
            nc.gpsimd.tensor_copy(ident16[:, :], ident[:, :]).then_inc(consts, 1)
            pool.wait_ge(ext_ready, 1)
            nc.gpsimd.partition_all_reduce(allx[:, 0:2], ext[:, 0:2], P, MAX).then_inc(ext_all, 1)
            nc.gpsimd.partition_all_reduce(allx[:, 2:3], ext[:, 2:3], P, ADD).then_inc(ext_all, 1)
            n, src = T // 2, wh
            pool.wait_ge(wh_copied, Q // 4 * HALVES)
            while n:
                nc.gpsimd.tensor_tensor(sq[:, T - n:T, :], src[:, 0:n, :], src[:, n:2 * n, :], ALU.add)\
                    .then_inc(mean_in, 1)
                src = sq[:, T - n:T, :]
                n //= 2
                pool.wait_ge(mean_in, T.bit_length() - 1 - n.bit_length())
            fast = is_fast(pool)
            with pool.If(fast == 1):
                pool.wait_ge(den_w_ready, 2)

                def pads(b, m):
                    for buf in range(2):
                        pool.wait_ge(masks_free, b * NS + m * 2 + buf + 1)
                        held()
                        nc.gpsimd.tensor_copy(den_pad[:, buf, :, :, 0:2],
                                              den_w[:, :, bass.ds((m * 2 + buf) * JT, JT), :])\
                            .then_inc(pad_ready, 1)

                def block_end(b, part):
                    links = 17

                    def tie(ins, k):
                        ins.then_inc(pool_c, 1)
                        pool.wait_ge(pool_c, b * links + k)
                        held()

                    def row_factors(pattern, **sizes):
                        return row_f[:, bass.ds(b * RT, RT), :].rearrange(pattern, **sizes)

                    def wide(ap):
                        return ap.unsqueeze(2).to_broadcast([P, RT, F])

                    if part == 0:
                        pool.dma_start(res, x_t[:, bass.ds(b * RT, RT), :]).then_inc(res_in, 16)
                        pool.wait_ge(round_act, b * RND + 2)
                        held()
                        tie(nc.gpsimd.tensor_scalar(den_end[:, :, :, :, 1], den_end[:, :, :, :, 1],
                                                    1.0 / LO, 0.0, ALU.mult, ALU.add), 1)
                        tie(nc.gpsimd.tensor_tensor(den_k[:, :, :, :], den_end[:, :, :, :, 0],
                                                    den_end[:, :, :, :, 1], ALU.add), 2)
                        for k in range(2):
                            ins = nc.gpsimd.tensor_tensor(
                                den_k[:, :, k, :], den_k[:, :, k, :],
                                row_factors("p (h t) k -> p t h k", h=2)[:, :, :, k], ALU.mult)
                            tie(ins, 3 + k)
                        tie(nc.gpsimd.tensor_tensor(
                            den_row[:, :, :].rearrange("p h t -> p t h"),
                            den_k[:, :, 0, :], den_k[:, :, 1, :], ALU.add), 5)
                        tie(nc.gpsimd.tensor_scalar(no_edge[:, :, :], den_row[:, :, :], 0.0, None,
                                                    ALU.is_equal), 6)
                        ins = nc.gpsimd.tensor_tensor(den_row[:, :, :], den_row[:, :, :],
                                                      no_edge[:, :, :], ALU.add)
                        ins.then_inc(den_ready, 1)
                    if part == 1:
                        pool.wait_ge(round_act, (b + 1) * RND + 1)
                        held()
                        tie(nc.gpsimd.tensor_scalar(end_lo, end_lo, 1.0 / LO, 0.0,
                                                    ALU.mult, ALU.add), 7)
                        tie(nc.gpsimd.tensor_tensor(end_lo, end_lo, ends[:, :, :, 0:F], ALU.add), 8)
                    if part == 2:
                        for k in range(2):
                            tie(nc.gpsimd.tensor_tensor(end_lo[:, :, k, :], end_lo[:, :, k, :],
                                                        wide(row_factors("p t k -> p t k")[:, :, k]),
                                                        ALU.mult), 9 + k)
                        nc.gpsimd.tensor_tensor(num, end_lo[:, :, 0, :], end_lo[:, :, 1, :], ALU.add)\
                            .then_inc(pool_c, 1)
                        pool.wait_ge(pool_c, b * links + 11)
                        pool.sem_inc(ends_free, 1)
                    if part == 3:
                        pool.wait_ge(recip_ready, b + 1)
                        held()
                        tie(nc.gpsimd.tensor_scalar(recip[:, :], recip[:, :], sc[:, 5:6], DTOP / VTOP,
                                                    ALU.mult, ALU.mult), 12)
                        tie(nc.gpsimd.tensor_tensor(num, num, wide(recip[:, :]), ALU.mult), 13)
                        tie(nc.gpsimd.tensor_tensor(
                            elu, mean_wh[:, :].unsqueeze(1).to_broadcast([P, RT, F]),
                            wide(no_edge[:, :, :].rearrange("p h t -> p (h t)")), ALU.mult), 14)
                        tie(nc.gpsimd.tensor_tensor(num, num, elu, ALU.add), 15)
                        nc.gpsimd.tensor_scalar(elu, num, 0.0, None, ALU.min).then_inc(elu_in, 1)
                    if part == 4:
                        pool.wait_ge(elu_out, b + 1)
                        held()
                        tie(nc.gpsimd.tensor_scalar(num, num, 0.0, -1.0, ALU.max, ALU.add), 16)
                        pool.wait_ge(res_in, b * 16 + 16)
                        held()
                        tie(nc.gpsimd.tensor_tensor(elu, elu, res, ALU.add), 17)
                        nc.gpsimd.tensor_tensor(num, num, elu, ALU.add).then_inc(res_done, 1)
                        pool.wait_ge(res_done, b + 1)
                        held()
                        pool.dma_start(out_t[:, bass.ds(b * RT, RT), :], num).then_inc(stored, 16)
                    if part == 5:
                        pool.wait_ge(stored, b * 16 + 16)
                        held()

                pool.sem_inc(ends_free, 1)
                def features(n, part):
                    k, tiles = n % 2, bass.ts(1 + n // 2, XT)
                    if part == 0:
                        nc.gpsimd.tensor_tensor(fscaled[0], wh[:, tiles, :],
                                                scaled[:, k, tiles].unsqueeze(2).to_broadcast([P, XT, F]),
                                                ALU.mult).then_inc(fsc_ready, 1)
                    else:
                        pool.wait_ge(fhi_ready, 3 + n)
                        nc.gpsimd.tensor_scalar(fscaled[1], feats[:, k, tiles, 0:F], -LO, 0.0, ALU.mult, ALU.add)\
                            .then_inc(feat_c, 1)
                        pool.wait_ge(feat_c, 2 * n + 1)
                        nc.gpsimd.tensor_tensor(feats[:, k, tiles, F:P], fscaled[1], fscaled[0], ALU.add)\
                            .then_inc(feat_c, 1)
                        pool.wait_ge(feat_c, 2 * n + 2)
                        pool.sem_inc(fts, 1)

                pool.wait_ge(scaled_ready, 2)
                pool.wait_ge(fts, 2)
                features(0, 0)
                for m in range(NP):
                    pads(0, m)
                    for n, at_step in enumerate(VALUE_STEPS):
                        if m == at_step // 2:
                            features(n, 1)
                            if n + 1 < ITEMS:
                                features(n + 1, 0)
                with pool.Fori(0, NB - 1) as b:
                    for m in range(NP):
                        pads(b + 1, m)
                        if m == 1:
                            block_end(b, 0)
                        elif m in (3, 4, 5, 13, 15):
                            block_end(b, {3: 1, 4: 2, 5: 3, 13: 4, 15: 5}[m])
                for part in range(6):
                    block_end(NB - 1, part)
            with pool.If(fast == 0):
                pool.sem_inc(gen_free, 1)
                with pool.Fori(0, T) as t:
                    pool.wait_ge(g_o, t + 2)
                    held()
                    pool.dma_start(out[bass.ds(t * P, P), :], gen_o).then_inc(g_st, 16)
                    pool.wait_ge(g_st, t * 16 + 16)
                    pool.sem_inc(gen_free, 1)

        @block.scalar
        def _(act):
            for g in range(XG):
                tiles = bass.ts(g, XT)
                act.wait_ge(centered, g + 1)
                nc.scalar.activation(sq[:, tiles, :], xa[:, tiles, :], ACT.Square).then_inc(sq_done, 1)
                for n in range(XQ // 4):
                    act.wait_ge(xT_done, g * (XQ // 4) + n + 1)
                    nc.scalar.activation(hT[:, bass.ts(g * (XQ // 4) + n, 512)],
                                         bank[(g * (XQ // 4) + n) % 2][:, :], ACT.Relu)\
                        .then_inc(relu_done, 1)
                act.wait_ge(var_ready, g + 1)
                nc.scalar.activation(stat[:, 2, tiles], stat[:, 1, tiles], ACT.Sqrt).then_inc(root_done, 1)
            act.wait_ge(sdT_pe, 1)
            nc.scalar.activation(sdT[:, :], end[:, 0:P], ACT.Copy).then_inc(sdT_ready, 1)
            act.wait_ge(scal, 1)
            nc.scalar.activation(e_pos[:, :], sd[:, 1, :], ACT.Exp, bias=sc[:, 0:1]).then_inc(exps, 1)
            nc.scalar.activation(e_neg[:, :], sd[:, 1, :], ACT.Exp, bias=sc[:, 1:2], scale=ALPHA)\
                .then_inc(exps, 1)
            act.wait_ge(rows_ready, 1)
            nc.scalar.activation(row_f[:, :, 0], stat[:, 4, :], ACT.Exp, scale=1 - ALPHA)\
                .then_inc(exps, 1)
            nc.scalar.activation(row_f[:, :, 1], stat[:, 5, :], ACT.Exp, scale=ALPHA - 1)\
                .then_inc(exps, 1)
            fast = is_fast(act)
            with act.If(fast == 1):
                for k in range(2):
                    act.wait_ge(fsc_ready, k + 1)
                    nc.scalar.activation(feats[:, k, 0:XT, 0:F], fscaled[k], ACT.Copy, scale=1 / LO)\
                        .then_inc(fhi_ready, 1)

                def value_part(n):
                    act.wait_ge(fsc_ready, 3 + n)
                    nc.scalar.activation(feats[:, n % 2, bass.ts(1 + n // 2, XT), 0:F], fscaled[0],
                                         ACT.Copy, scale=1 / LO).then_inc(fhi_ready, 1)

                def convert(slot, part, turn_no, step):
                    act.wait_ge(adj_in[slot], turn_no * 16 + 16)
                    if step is not None:
                        act.wait_ge(mask_used, (step + 1) * JT)
                    nc.scalar.activation(mask[:, part % 2], slots[:, slot, :, bass.ts(part, JP)],
                                         ACT.Sign, bias=minus_half).then_inc(adj_used, 1)

                def negatives(g, buf, n):
                    act.wait_ge(coded, (g + 1) * JT)
                    act.wait_ge(masks_free, g + 1)
                    nc.scalar.activation(m_neg[:, buf, 0:n], code[:, buf, 0:n], ACT.Relu, scale=-1.0)\
                        .then_inc(neg_act, 1)

                def copy_sums(b):
                    act.wait_ge(sums_done, b + 1)
                    act.wait_ge(round_pe, b * RND + 1)
                    for h in range(2):
                        nc.scalar.activation(acc_sb[:, 0, bass.ts(h, 512)], acc[0][h][:, :], ACT.Copy)\
                            .then_inc(acc_act, 1)

                def copy_den(b):
                    act.wait_ge(masks_free, (b + 1) * NS + 2)
                    nc.scalar.activation(den_sb, den[:, :], ACT.Copy).then_inc(acc_act, 1)

                def copy_round(b, r):
                    act.wait_ge(round_pe, b * RND + r + 2)
                    if r == 0:
                        act.wait_ge(ends_free, b + 1)
                        rows = end[:, :].rearrange("p (t g c) -> p (t g) c", t=4, g=4)[:, :, 0:2]
                        nc.scalar.activation(den_end[:, :, :, :, :].rearrange("p t k h c -> p (t k h) c"),
                                             rows, ACT.Copy).then_inc(round_act, 1)
                    else:
                        nc.scalar.activation(ends[:, 2 * r - 2:2 * r, :, :].rearrange("p t k c -> p (t k c)"),
                                             end[:, :], ACT.Copy).then_inc(round_act, 1)

                def exp_end(b):
                    act.wait_ge(elu_in, b + 1)
                    nc.scalar.activation(elu, elu, ACT.Exp).then_inc(elu_out, 1)

                LEAD = 2
                TURNS = NS // CYC
                for r in range(LEAD):
                    convert(r // SPL, r % SPL, 0, None)

                def turn(b, m, ended=None, last=False, items=False):
                    for r in range(CYC):
                        g = b * NS + m * CYC + r
                        if not (last and r + LEAD >= CYC):
                            rr = (r + LEAD) % CYC
                            convert(rr // SPL, rr % SPL, b * TURNS + m + (r + LEAD) // CYC, g)
                        if items and m * CYC + r in VALUE_STEPS:
                            value_part(VALUE_STEPS.index(m * CYC + r))
                        if ended is not None:
                            if r == 0:
                                copy_sums(ended)
                            if 2 <= r < 2 + RND:
                                copy_round(ended, r - 2)
                        negatives(g, r % 2, WA_END if ended is not None and r in LIGHT else WA)
                        if ended is not None and r == 0:
                            copy_den(ended)

                turn(0, 0, items=True)
                turn(0, 1, items=True)
                turn(0, 2, items=True)
                with act.Fori(3, TURNS) as m:
                    turn(0, m)
                with act.Fori(0, NB - 2) as b:
                    turn(b + 1, 0, ended=b)
                    with act.Fori(1, TURNS - 1) as m:
                        turn(b + 1, m)
                    exp_end(b)
                    turn(b + 1, TURNS - 1)
                turn(NB - 1, 0, ended=NB - 2)
                with act.Fori(1, TURNS - 1) as m:
                    turn(NB - 1, m)
                exp_end(NB - 2)
                turn(NB - 1, TURNS - 1, last=True)
                copy_sums(NB - 1)
                copy_den(NB - 1)
                for r in range(RND):
                    copy_round(NB - 1, r)
                exp_end(NB - 1)
            with act.If(fast == 0):
                with act.Fori(0, T) as t:
                    act.wait_ge(g_score, t + 2)
                    nc.scalar.activation(gen_p, gen_p, ACT.Exp, bias=g1[:, 1:2], accum_out=g1[:, 2:3])\
                        .then_inc(g_exp, 1)
                    act.wait_ge(g_n, t + 1)
                    nc.scalar.activation(gen_e, gen_e, ACT.Exp).then_inc(g_e, 1)

        @block.vector
        def _(v):
            chain = [0]

            def link(ins):
                chain[0] += 1
                ins.then_inc(dve, 1)
                v.wait_ge(dve, chain[0])

            def over_f(ap):
                return ap.unsqueeze(2).to_broadcast([*ap.shape, F])

            nc.vector.memset(minus_half, -0.5).then_inc(consts, 1)
            v.wait_ge(wT_done, 1)
            nc.vector.tensor_copy(wT[:, 0:F], end[0:F, 0:F]).then_inc(wTc, 1)
            nc.vector.tensor_copy(wT[:, F:P], end[0:F, 0:F]).then_inc(wTc, 1)
            link(nc.vector.tensor_tensor(w_sq, w2[:, 0:F], w2[:, 0:F], ALU.mult))
            link(nc.vector.tensor_reduce(ext[:, 2:3], w_sq, AX.X, ALU.add))

            def centre(g):
                tiles = bass.ts(g, XT)
                v.wait_ge(x_in[g], 16)
                link(nc.vector.tensor_reduce(stat[:, 0, tiles], xa[:, tiles, :], AX.X, ALU.add))
                link(nc.vector.tensor_scalar(stat[:, 0, tiles], stat[:, 0, tiles], 1.0 / F, None, ALU.mult))
                nc.vector.tensor_tensor(xa[:, tiles, :], xa[:, tiles, :], over_f(stat[:, 0, tiles]),
                                        ALU.subtract).then_inc(centered, 1)

            def root(g):
                tiles = bass.ts(g, XT)
                v.wait_ge(sq_done, g + 1)
                link(nc.vector.tensor_reduce(stat[:, 0, tiles], sq[:, tiles, :], AX.X, ALU.add))
                nc.vector.tensor_scalar(stat[:, 1, tiles], stat[:, 0, tiles], 1.0 / F, EPS,
                                        ALU.mult, ALU.add).then_inc(var_ready, 1)
                v.wait_ge(var_ready, g + 1)
                v.wait_ge(root_done, g + 1)
                link(nc.vector.reciprocal(stat[:, 3, tiles], stat[:, 2, tiles]))
                link(nc.vector.tensor_tensor(stat[:, 4, tiles], stat[:, 3, tiles], stat[:, 3, tiles],
                                             ALU.mult))
                link(nc.vector.tensor_tensor(stat[:, 4, tiles], stat[:, 4, tiles], stat[:, 1, tiles],
                                             ALU.mult))
                link(nc.vector.tensor_scalar(stat[:, 4, tiles], stat[:, 4, tiles], -0.5, 1.5,
                                             ALU.mult, ALU.add))
                link(nc.vector.tensor_tensor(rstd[:, tiles], stat[:, 3, tiles], stat[:, 4, tiles],
                                             ALU.mult))

            rstd_v = rstd[:, :].rearrange("p (q h) -> p q h", h=HALVES)
            whx_v = big[:, wh0:wh0 + T * FX].rearrange("p (q h c) -> p q h c", h=HALVES, c=FX)

            def take(g):
                for n in range(g * (XQ // 4), (g + 1) * (XQ // 4)):
                    for h in range(HALVES):
                        v.wait_ge(wh_pe, n * HALVES + h + 1)
                        nc.vector.tensor_tensor(
                            whx_v[:, 4 * n:4 * n + 4, h, :],
                            bank[2 + 2 * (n % 2) + h][:, 0:4 * FX].rearrange("p (q c) -> p q c", q=4),
                            rstd_v[:, 4 * n:4 * n + 4, h].unsqueeze(2).to_broadcast([P, 4, FX]),
                            ALU.mult).then_inc(wh_copied, 1)

            centre(0)
            v.wait_ge(wa_done, 1)
            nc.vector.tensor_copy(w2[:, F:FX], bank[6][:, 0:2]).then_inc(wac, 1)
            centre(1)
            for g in range(XG):
                root(g)
                if g + 2 < XG:
                    centre(g + 2)
                take(g)
            v.wait_ge(wh_copied, Q // 4 * HALVES)
            nc.vector.tensor_copy(sd[:, :, :], whx[:, :, F:FX].rearrange("p t k -> p k t"))\
                .then_inc(sd_ready, 1)
            link(nc.vector.tensor_reduce(ext[:, 0:1], whx[:, :, F + 1], AX.X, ALU.max))
            v.wait_ge(sd_ready, 1)
            link(nc.vector.tensor_scalar(neg_d[:, :], sd[:, 1, :], -1.0, None, ALU.mult))
            nc.vector.tensor_reduce(ext[:, 1:2], neg_d[:, :], AX.X, ALU.max).then_inc(ext_ready, 1)
            v.wait_ge(ext_all, 2)
            nc.vector.tensor_scalar(sc[:, 1:2], allx[:, 0:1], -ALPHA, None, ALU.mult)
            nc.vector.tensor_scalar(sc[:, 0:1], allx[:, 0:1], -1.0, None, ALU.mult).then_inc(scal, 1)
            link(nc.vector.tensor_tensor(sc[:, 2:3], allx[:, 0:1], allx[:, 1:2], ALU.add))
            link(nc.vector.tensor_scalar(sc[:, 3:4], sc[:, 2:3], SPAN, None, ALU.is_le))
            link(nc.vector.tensor_scalar(sc[:, 4:5], allx[:, 2:3], 1e-20, None, ALU.is_ge))
            link(nc.vector.tensor_tensor(sc[:, 3:4], sc[:, 3:4], sc[:, 4:5], ALU.mult))
            link(nc.vector.tensor_scalar(sc[:, 4:5], allx[:, 2:3], 1e20, None, ALU.is_le))
            nc.vector.tensor_tensor(flag[:, :], sc[:, 3:4], sc[:, 4:5], ALU.mult).then_inc(flag_ready, 1)
            link(nc.vector.tensor_scalar(sc[:, 5:6], allx[:, 2:3], 0.25 * float(F) ** 0.5,
                                         0.5 * float(F) ** 0.5, ALU.mult, ALU.add))
            link(nc.vector.reciprocal(sc[:, 6:7], sc[:, 5:6]))
            nc.vector.tensor_scalar(stat[:, 4, :], sd[:, 0, :], allx[:, 0:1], 0.0, ALU.add, ALU.min)
            nc.vector.tensor_scalar(stat[:, 5, :], sd[:, 0, :], allx[:, 0:1], 0.0,
                                    ALU.add, ALU.max).then_inc(rows_ready, 1)
            chained = chain[0]
            fast = is_fast(v)
            with v.If(fast == 1):
                for k, e in enumerate((e_pos, e_neg)):
                    v.wait_ge(exps, k + 1)
                    nc.vector.tensor_scalar(scaled[:, k, :], e[:, :], sc[:, 6:7], VTOP * LO,
                                            ALU.mult, ALU.mult).then_inc(scaled_ready, 1)
                    v.wait_ge(scaled_ready, k + 1)
                    nc.vector.tensor_tensor(fscaled[k], wh[:, 0:XT, :], over_f(scaled[:, k, 0:XT]),
                                            ALU.mult).then_inc(fsc_ready, 1)
                for k, e in enumerate((e_pos, e_neg)):
                    link(nc.vector.tensor_scalar(den_w[:, k, :, 0], e[:, :], DTOP, None, ALU.mult))
                    link(nc.vector.tensor_scalar(stat[:, k, :], e[:, :], DTOP * LO, None, ALU.mult))
                    nc.vector.scalar_tensor_tensor(den_w[:, k, :, 1], den_w[:, k, :, 0], -LO,
                                                   stat[:, k, :], ALU.mult, ALU.add)\
                        .then_inc(den_w_ready, 1)
                for k in range(2):
                    v.wait_ge(fhi_ready, k + 1)
                    v.wait_ge(fsc_ready, k + 1)
                    nc.vector.scalar_tensor_tensor(feats[:, k, 0:XT, F:P], feats[:, k, 0:XT, 0:F], -LO,
                                                   fscaled[k], ALU.mult, ALU.add).then_inc(fts, 1)
                v.wait_ge(mean_pe, 1)
                nc.vector.tensor_copy(mean_wh[:, :], end[:, 0:F]).then_inc(mean_ready, 1)
                v.wait_ge(exps, 4)
                v.wait_ge(rows_in, 16)

                def encode(b, sj, buf, u, early):
                    g = b * NS + sj
                    if u == 0:
                        v.wait_ge(neg_act, g + 1)
                        if not early:
                            v.wait_ge(masks_dve, g - 1)
                    v.wait_ge(mask_used, g * JT + u + 1)
                    nc.vector.scalar_tensor_tensor(
                        code[:, buf, bass.ts(u, IB)], s_rows[:, bass.ds(b * IB, IB)],
                        neg_d[:, bass.ds(sj * JT + u, 1)], tr[u][:, :], ALU.is_gt, ALU.subtract)\
                        .then_inc(coded, 1)

                def masks(g, buf, n=WA):
                    v.wait_ge(masks_free, g + 1)
                    v.wait_ge(coded, (g + 1) * JT)
                    nc.vector.tensor_scalar(m_pos[:, buf, :], code[:, buf, :], 0.0, None, ALU.is_equal)
                    nc.vector.tensor_scalar(m_neg[:, buf, n:W], code[:, buf, n:W], -1.0, None,
                                            ALU.is_equal).then_inc(masks_dve, 1)

                def copy_sums(b, part):
                    if part == 0:
                        v.wait_ge(sums_done, b + 1)
                        v.wait_ge(round_pe, b * RND + 1)
                    nc.vector.tensor_copy(acc_sb[:, 1, bass.ts(part, 512)], acc[1][part][:, :])\
                        .then_inc(acc_dve, 1)

                def reciprocals(b):
                    v.wait_ge(den_ready, b + 1)
                    nc.vector.reciprocal(recip[:, :], den_row[:, :, :].rearrange("p h t -> p (h t)"))\
                        .then_inc(recip_ready, 1)

                def step(b, sj, buf, ended=None, sums=False, first=False, early=False):
                    g = b * NS + sj
                    encode(b, sj, buf, 0, early)
                    if sums:
                        copy_sums(ended, 0)
                    if not first:
                        masks(g - 1, 1 - buf, WA_END if ended is not None and sj - 1 in LIGHT else WA)
                    if sums:
                        copy_sums(ended, 1)
                    encode(b, sj, buf, 1, early)

                PEEL = LIGHT[-1] // 2 + 1
                step(0, 0, 0, first=True, early=True)
                step(0, 1, 1, early=True)
                v.wait_ge(rows_in2, 16)
                with v.Fori(1, NP) as m:
                    step(0, m * 2, 0)
                    step(0, m * 2 + 1, 1)
                with v.Fori(0, NB - 1) as b:
                    step(b + 1, 0, 0)
                    for sj in range(1, 2 * PEEL):
                        step(b + 1, sj, sj % 2, ended=b, sums=(sj == 1))
                    reciprocals(b)
                    with v.Fori(PEEL, NP) as m:
                        step(b + 1, m * 2, 0)
                        step(b + 1, m * 2 + 1, 1)
                masks(NB * NS - 1, 1)
                for part in range(2):
                    copy_sums(NB - 1, part)
                reciprocals(NB - 1)
            with v.If(fast == 0):
                v.wait_ge(mean_pe, 1)
                v.wait_ge(g_rows, 16)
                v.sem_inc(g_score, 1)
                v.sem_inc(g_o, 1)
                v.sem_inc(g_trc, 1)
                GCH = 12
                with v.Fori(0, T) as t:
                    def tie(ins, k):
                        ins.then_inc(dve, 1)
                        v.wait_ge(dve, chained + t * GCH + k)

                    v.wait_ge(g_in, t * 16 + 16)
                    v.wait_ge(g_pv, t + 1)
                    tie(nc.vector.tensor_scalar(gen_p, gen_adj, 0.0, OFF, ALU.is_le, ALU.mult), 1)
                    tie(nc.vector.tensor_tensor(gen_p, gen_p, d_rows[:, :], ALU.add), 2)
                    tie(nc.vector.tensor_reduce(g1[:, 0:1], gen_p, AX.X, ALU.max), 3)
                    s_col = sd[:, 0, bass.ds(t, 1)]
                    tie(nc.vector.tensor_scalar(gen_p, gen_p, s_col, None, ALU.add), 4)
                    tie(nc.vector.tensor_scalar(g1[:, 0:1], g1[:, 0:1], s_col, None, ALU.add), 5)
                    tie(nc.vector.scalar_tensor_tensor(g1[:, 3:4], g1[:, 0:1], ALPHA, g1[:, 0:1],
                                                       ALU.mult, ALU.max), 6)
                    tie(nc.vector.tensor_scalar(g1[:, 1:2], g1[:, 3:4], -1.0, None, ALU.mult), 7)
                    nc.vector.scalar_tensor_tensor(gen_p, gen_p, ALPHA, gen_p, ALU.mult, ALU.max)\
                        .then_inc(g_score, 1)
                    for c in range(T // 4):
                        v.wait_ge(g_tr, t * (T // 4) + c + 1)
                        nc.vector.tensor_copy(gen_pT[:, bass.ts(c % 2, 512)], bank[c % 2][:, :])\
                            .then_inc(g_trc, 1)
                    v.wait_ge(g_pv, t + 2)
                    v.wait_ge(g_exp, t + 1)
                    tie(nc.vector.reciprocal(g1[:, 4:5], g1[:, 2:3]), 8)
                    v.wait_ge(gen_free, t + 1)
                    tie(nc.vector.tensor_scalar(gen_o, bank[2][:, 0:F], g1[:, 4:5], None, ALU.mult), 9)
                    nc.vector.tensor_scalar(gen_e, gen_o, 0.0, None, ALU.min).then_inc(g_n, 1)
                    v.wait_ge(g_x, t * 16 + 16)
                    tie(nc.vector.scalar_tensor_tensor(gen_o, gen_o, 0.0, gen_x, ALU.max, ALU.add), 10)
                    v.wait_ge(g_e, t + 1)
                    tie(nc.vector.tensor_scalar(gen_e, gen_e, -1.0, None, ALU.add), 11)
                    tie(nc.vector.tensor_tensor(gen_o, gen_e, gen_o, ALU.add), 12)
                    nc.vector.tensor_copy(g1[:, 5:6], g1[:, 4:5]).then_inc(g_o, 1)

        @block.tensor
        def _(pe):
            pe.wait_ge(consts, 2)
            pe.wait_ge(w_in, 64)
            nc.tensor.transpose(end[0:F, 0:F], w2[0:F, 0:F], ident[0:F, 0:F]).then_inc(wT_done, 1)
            pe.wait_ge(wTc, 2)
            nc.tensor.matmul(bank[6][:, 0:2], wT[:, :], a2[:, :], start=True, stop=True)\
                .then_inc(wa_done, 1)

            def turn_x(g):
                pe.wait_ge(centered, g + 1)
                for n in range(g * (XQ // 4), (g + 1) * (XQ // 4)):
                    if n >= 2:
                        pe.wait_ge(relu_done, n - 1)
                    for u in range(4):
                        q = 4 * n + u
                        last = nc.tensor.transpose(bank[n % 2][:, bass.ts(u, P)],
                                                   xa[:, 2 * q:2 * q + 2, :].rearrange("p t f -> p (t f)"),
                                                   ident[:, :])
                    last.then_inc(xT_done, 1)

            turn_x(0)
            pe.wait_ge(wac, 1)
            for g in range(XG):
                if g + 1 < XG:
                    turn_x(g + 1)
                for n in range(g * (XQ // 4), (g + 1) * (XQ // 4)):
                    pe.wait_ge(relu_done, n + 1)
                    for h in range(HALVES):
                        hp = slice(h * F, (h + 1) * F)
                        if n >= 2:
                            pe.wait_ge(wh_copied, (n - 2) * HALVES + h + 1)
                        for u in range(4):
                            last = nc.tensor.matmul(bank[2 + 2 * (n % 2) + h][:, bass.ts(u, FX)],
                                                    hT[hp, bass.ts(4 * n + u, P)], w2[hp, :],
                                                    start=True, stop=True)
                        last.then_inc(wh_pe, 1)
            pe.wait_ge(sd_ready, 1)
            nc.tensor.transpose(end[:, 0:P], sd[:, :, :].rearrange("p k t -> p (k t)"), ident[:, :])\
                .then_inc(sdT_pe, 1)
            pe.wait_ge(mean_in, T.bit_length() - 1)
            pe.wait_ge(sdT_ready, 1)
            nc.tensor.matmul(end[:, 0:F], ones_n[:, :], sq[:, T - 1, :], start=True, stop=True)\
                .then_inc(mean_pe, 1)
            fast = is_fast(pe)
            with pe.If(fast == 1):
                nc.tensor.transpose(tr[0][:, 0:P], ident16[:, :], ident16[:, :]).then_inc(neg_act, 2)
                nc.tensor.transpose(tr[0][:, 0:P], ident16[:, :], ident16[:, :]).then_inc(masks_free, 2)

                def transposes(g, buf, u, first=False):
                    if u == 0:
                        pe.wait_ge(adj_used, g + 1)
                    if not first:
                        pe.wait_ge(coded, (g - 1) * JT + u + 1)
                    for r in range(RT):
                        last = nc.tensor.transpose(tr[u][:, bass.ts(r, P)],
                                                   mask[:, buf, r, bass.ts(u, P)], ident16[:, :])
                    last.then_inc(mask_used, 1)

                def products(b, sj, buf, start, stop, ended):
                    g = b * NS + sj
                    pe.wait_ge(masks_dve, g + 1)
                    pe.wait_ge(neg_act, g + 3)
                    order = [(u, k) for u in range(JT) for k in range(2)]
                    if start:
                        order = [(u, k) for k in range(2) for u in range(JT)]
                    for u, k in order:
                        for h in range(2):
                            if ended is not None and u == 0:
                                if k == 0:
                                    pe.wait_ge(acc_act, 3 * ended + h + 1)
                                else:
                                    pe.wait_ge(acc_dve, 2 * ended + h + 1)
                            last = nc.tensor.matmul(acc[k][h][:, :],
                                                    feats[:, k, bass.ds(sj * JT + u, 1), :]
                                                    .rearrange("p t c -> p (t c)"),
                                                    (m_pos, m_neg)[k][:, buf, u * IB + h * 512:
                                                                      u * IB + (h + 1) * 512],
                                                    start=start and u == 0, stop=stop and u == JT - 1)
                    if stop:
                        last.then_inc(sums_done, 1)
                    if ended is not None:
                        pe.wait_ge(acc_act, 3 * ended + 3)
                    pe.wait_ge(pad_ready, g + 1)
                    for u in range(JT):
                        s0, s1 = start and u == 0, stop and u == JT - 1
                        for k, m in enumerate((m_pos, m_neg)):
                            for h in range(2):
                                p0 = (2 * k + h) * DW
                                last = nc.tensor.matmul(den[p0:p0 + DW, :], den_pad[:, buf, k, u, :],
                                                        m[:, buf, u * IB + h * 512:u * IB + (h + 1) * 512],
                                                        start=s0, stop=s1, tile_position=(0, p0))
                    last.then_inc(masks_free, 1)

                def end_round(b, r):
                    if r == 0:
                        pe.wait_ge(acc_act, 3 * b + 3)
                        pe.wait_ge(acc_dve, 2 * b + 2)
                    pe.wait_ge(round_act, b * RND + r + 1)
                    for n in range(4):
                        if r == 0:
                            src = den_sb[:, bass.ts(n, P)]
                        else:
                            src = acc_sb[:, n % 2, bass.ts(2 * (r - 1) + n // 2, P)]
                        last = nc.tensor.transpose(end[:, bass.ts(n, P)], src, ident[:, :])
                    last.then_inc(round_pe, 1)

                def step(b, sj, buf, start=False, stop=False, ended=None, left=2):
                    g = b * NS + sj
                    if left >= 1:
                        transposes(g + 1, 1 - buf, 1)
                    if left >= 2:
                        transposes(g + 2, buf, 0)
                    products(b, sj, buf, start, stop, ended)

                transposes(0, 0, 0, first=True)
                transposes(0, 0, 1, first=True)
                transposes(1, 1, 0)
                pe.sem_inc(round_pe, 1)
                pe.sem_inc(round_act, 1)
                pe.wait_ge(fts, 2)
                step(0, 0, 0, start=True)
                step(0, 1, 1)
                for g in range(XG):
                    if g:
                        pe.wait_ge(fts, 2 * g + 2)
                    with pe.Fori(max(g * (NP // XG), 1), min((g + 1) * (NP // XG), NP - 1)) as m:
                        step(0, m * 2, 0)
                        step(0, m * 2 + 1, 1)
                step(0, NS - 2, 0)
                step(0, NS - 1, 1, stop=True)

                def block_steps(b, ended, left):
                    for sj in range(2 * (RND + 1) // 2):
                        step(b, sj, sj % 2, start=(sj == 0), ended=ended if sj == 0 else None)
                        if sj < RND:
                            end_round(ended, sj)
                    with pe.Fori((RND + 1) // 2, NP - 1) as m:
                        step(b, m * 2, 0)
                        step(b, m * 2 + 1, 1)
                    step(b, NS - 2, 0, left=min(left + 1, 2))
                    step(b, NS - 1, 1, stop=True, left=left)

                with pe.Fori(0, NB - 2) as b:
                    block_steps(b + 1, b, 2)
                block_steps(NB - 1, NB - 2, 0)
                for r in range(RND):
                    end_round(NB - 1, r)
            with pe.If(fast == 0):
                pe.sem_inc(g_pv, 1)
                with pe.Fori(0, T) as t:
                    pe.wait_ge(g_exp, t + 1)
                    pe.wait_ge(g_o, t + 1)

                    def turn_p(c):
                        pe.wait_ge(g_trc, t * (T // 4) + max(c - 2, 0) + (c > 1) + 1)
                        for u in range(4):
                            last = nc.tensor.transpose(bank[c % 2][:, bass.ts(u, P)],
                                                       gen_p[:, bass.ts(4 * c + u, P)], ident[:, :])
                        last.then_inc(g_tr, 1)

                    turn_p(0)
                    for c in range(T // 4):
                        if c + 1 < T // 4:
                            turn_p(c + 1)
                        pe.wait_ge(g_trc, t * (T // 4) + c + 2)
                        for u in range(4):
                            j = 4 * c + u
                            last = nc.tensor.matmul(bank[2][:, 0:F],
                                                    gen_pT[:, (c % 2) * 512 + u * P:(c % 2) * 512 + (u + 1) * P],
                                                    wh[:, j, :], start=(j == 0), stop=(j == T - 1))
                    last.then_inc(g_pv, 1)


_INS = ["x", "adj", "L0_gnn_W", "L0_gnn_a"]


def kernel(**inputs):
    import numpy as _np
    import concourse.bacc as _bacc
    from concourse import mybir as _mybir
    from concourse.bass_utils import run_bass_kernel_spmd as _run

    nc = _bacc.Bacc("TRN2", target_bir_lowering=False, num_devices=1)
    arrays, args = {}, []
    for name in _INS:
        arr = _np.ascontiguousarray(inputs[name])
        arrays[f"in_{name}"] = arr
        args.append(nc.dram_tensor(f"in_{name}", arr.shape, _mybir.dt.from_np(arr.dtype),
                                   kind="ExternalInput").ap())
    shape = arrays["in_x"].shape
    args.append(nc.dram_tensor("out_x", shape, _mybir.dt.float32, kind="ExternalOutput").ap())
    gat_preln_program(nc, *args)
    r = _run(nc, [arrays], core_ids=[0])
    return r.results[0]["out_x"]
```

```python
import concourse.bass as bass
from concourse import mybir
from contextlib import ExitStack


def gat_preln_program(nc, x, adj, w, a, out):
    fp32 = mybir.dt.float32
    fp16 = mybir.dt.float16
    i32 = mybir.dt.int32
    ALU = mybir.AluOpType
    ACT = mybir.ActivationFunctionType
    AX = mybir.AxisListType
    MAX = bass.bass_isa.ReduceOp.max
    ADD = bass.bass_isa.ReduceOp.add

    P = 128
    N, F = x.shape
    T = N // P
    HALVES = P // F
    ALPHA = 0.2
    EPS = 1e-5
    SPAN = 8.5
    LO = 2048.0
    VTOP = 32000.0
    DTOP = 16384.0
    OFF = -1.0e38

    IB = 1024
    NB = N // IB
    RT = IB // P
    JC = 512
    JP = 256
    JT = JP // P
    NS = N // JP
    SLOTS = 4
    SPL = JC // JP
    CYC = SLOTS * SPL
    LEAD = 2
    W = JT * IB
    WA = 1440
    WA_END = WA - 384
    DW = 32
    RND = 1 + RT // 2
    GAP = 3
    COPIES = tuple(range(2, 2 + GAP * RND, GAP))
    LIGHT = (0, *COPIES)
    END_TURNS = -(-(COPIES[-1] + 2) // CYC)
    JOIN = COPIES[-1] // 2
    ITEMS = 2 * 3
    VALUE_STEPS = range(1, NS - CYC, 4)
    EXP_STEP = NS - CYC
    NP = NS // 2

    XG = 4
    XT = T // XG
    XQ = XT // HALVES
    FX = F + 2

    x_t = x.rearrange("(t p) f -> p t f", p=P)
    out_t = out.rearrange("(t p) f -> p t f", p=P)
    adj_t = adj.rearrange("(t p) j -> p t j", p=P)

    sd_dram = nc.dram_tensor("sd_rows", [2, N], fp32, kind="Internal").ap()

    ctx = ExitStack()
    with ctx:
        def sb(name, shape, dt=fp32):
            return ctx.enter_context(nc.sbuf_tensor(name, shape, dt))

        def sem(name):
            return ctx.enter_context(nc.semaphore(name))

        ring = sb("ring", [P, SLOTS * RT * JC], i32)
        slots = ring[:, :].rearrange("p (s t j) -> p s t j", s=SLOTS, t=RT)
        gen_adj = ring[:, 0:N]
        s_rows = sb("s_rows", [P, N])
        d_rows = s_rows
        feat = sb("feat", [P, 2 * T * P], fp16)
        feats = feat[:, :].rearrange("p (k t c) -> p k t c", k=2, t=T)
        gen_p = feat[:, :].bitcast(fp32)
        den_w = sb("den_w", [P, 2, T, 2], fp16)
        den_pad = sb("den_pad", [P, 2, 2, JT, DW], fp16)
        mask = sb("mask", [P, 2, RT, JP], fp16)
        big = sb("big", [P, 13 * 1024])
        hT = big[:, 0:T // HALVES * P]
        xa = feat[:, :].bitcast(fp32)[:, 0:T * F].rearrange("p (t f) -> p t f", t=T)
        sq = feat[:, :].bitcast(fp32)[:, T * F:2 * T * F].rearrange("p (t f) -> p t f", t=T)
        wh0 = 3 * W
        whx = big[:, wh0:wh0 + T * FX].rearrange("p (t c) -> p t c", c=FX)
        wh = whx[:, :, 0:F]
        tail0 = wh0 + T * FX
        fscaled = [big[:, tail0 + n * XT * F:tail0 + (n + 1) * XT * F]
                   .rearrange("p (t f) -> p t f", t=XT) for n in range(2)]
        sums8 = big[:, tail0 + 2 * XT * F:tail0 + 2 * XT * F + 512].rearrange("p (n f) -> p n f", f=F)
        gen_pT = big[:, tail0:tail0 + 2 * 512]
        gen_x = big[:, tail0 + 1024:tail0 + 1024 + F]
        gen_o = big[:, tail0 + 1088:tail0 + 1088 + F]
        gen_e = big[:, tail0 + 1152:tail0 + 1152 + F]
        big16 = big[:, :].bitcast(fp16)
        code = big16[:, 0:2 * W].rearrange("p (b w) -> p b w", b=2)
        m_pos = big16[:, 2 * W:4 * W].rearrange("p (b w) -> p b w", b=2)
        m_neg = big16[:, 4 * W:6 * W].rearrange("p (b w) -> p b w", b=2)
        fast0 = 3 * W
        acc_sb = big[:, fast0:fast0 + 2 * IB].rearrange("p (k i) -> p k i", k=2)
        den_sb = big[:, fast0 + 2 * IB:fast0 + 2 * IB + 512]
        at = fast0 + 2 * IB + 512
        ends = big[:, at:at + 2048].rearrange("p (t k c) -> p t k c", t=RT, k=2)
        end_lo = ends[:, :, :, F:P]
        at2 = at + 2048
        num = big[:, at2:at2 + 512].rearrange("p (t f) -> p t f", t=RT)
        elu = big[:, at2 + 512:at2 + 1024].rearrange("p (t f) -> p t f", t=RT)
        res = big[:, at2 + 1024:at2 + 1536].rearrange("p (t f) -> p t f", t=RT)

        w2 = sb("w2", [P, HALVES * FX])
        a2 = sb("a2", [F, 2])
        wT = sb("wT", [F, P])
        ident = sb("ident", [P, P])
        ident16 = sb("ident16", [P, P], fp16)
        ones_n = sb("ones_n", [P, P])
        mean_wh = sb("mean_wh", [P, F])
        stat = sb("stat", [P, 6, T])
        rstd = sb("rstd", [P, T])
        sdT = sb("sdT", [P, P])
        sd = sb("sd", [P, 2, T])
        neg_d = sb("neg_d", [P, T])
        ext = sb("ext", [P, 4])
        allx = sb("allx", [P, 4])
        sc = sb("sc", [P, 12])
        flag = sb("flag", [P, 1], i32)
        e_pos = sb("e_pos", [P, T])
        e_neg = sb("e_neg", [P, T])
        scaled = sb("scaled", [P, 2, T])
        row_f = sb("row_f", [P, T, 2])
        den_end = sb("den_end", [P, 4, 2, 2, 2])
        den_k = sb("den_k", [P, 4, 2, 2])
        den_row = sb("den_row", [P, 2, 4])
        no_edge = sb("no_edge", [P, 2, 4])
        recip = sb("recip", [P, RT])
        factors = sb("factors", [P, RT, 2])
        g1 = sb("g1", [P, 8])

        minus_half = sc[:, 11:12]
        w_sq = hT[:, 0:HALVES * FX]

        bank = [ctx.enter_context(nc.psum_tensor(f"bank{k}", [P, 512], fp32)) for k in range(8)]
        tr = [bank[k][:, :].bitcast(fp16) for k in (0, 1)]
        acc = [[bank[2], bank[3]], [bank[4], bank[5]]]
        den = bank[6]
        end = bank[7]

        x_in, w_in = [sem(f"x_in{k}") for k in range(XG)], sem("w_in")
        adj_in = [sem(f"adj_in{k}") for k in range(SLOTS)]
        adj_used = sem("adj_used")
        mask_used = sem("mask_used")
        coded = sem("coded")
        neg_act = sem("neg_act")
        masks_dve = sem("masks_dve")
        masks_free = sem("masks_free")
        pad_ready = sem("pad_ready")
        acc_act, acc_dve = sem("acc_act"), sem("acc_dve")
        sums_done = sem("sums_done")
        round_pe = sem("round_pe")
        round_act = sem("round_act")
        ends_free = sem("ends_free")
        den_ready, recip_ready = sem("den_ready"), sem("recip_ready")
        pool_c = sem("pool_c")
        elu_in, elu_out = sem("elu_in"), sem("elu_out")
        last_x, last_den, last_pe, last_low = sem("last_x"), sem("last_den"), sem("last_pe"), sem("last_low")
        last_min, last_exp, last_rows, last_out = (sem("last_min"), sem("last_exp"), sem("last_rows"),
                                                   sem("last_out"))
        res_in, res_done, stored = sem("res_in"), sem("res_done"), sem("stored")
        dve, pool_s = sem("dve"), sem("pool_s")
        w_zero, x_mean, sums8_in = sem("w_zero"), sem("x_mean"), sem("sums8_in")
        mean_in = sem("mean_in")
        pool_waits = sem("pool_waits")
        gen_free = sem("gen_free")
        consts, centered, sq_done = sem("consts"), sem("centered"), sem("sq_done")
        var_ready, root_done, xT_done, relu_done = (sem("var_ready"), sem("root_done"), sem("xT_done"),
                                                    sem("relu_done"))
        wT_done, wTc, wa_done, wac = sem("wT_done"), sem("wTc"), sem("wa_done"), sem("wac")
        wh_pe, wh_copied = sem("wh_pe"), sem("wh_copied")
        sd_ready, sdT_pe, sdT_ready, sd_out = sem("sd_ready"), sem("sdT_pe"), sem("sdT_ready"), sem("sd_out")
        rows_in = sem("rows_in")
        fsc1_ready = sem("fsc1_ready")
        den_w_ready, feat_c = sem("den_w_ready"), sem("feat_c")
        scaled_ready = sem("scaled_ready")
        ext_ready, ext_all, scal, exps = sem("ext_ready"), sem("ext_all"), sem("scal"), sem("exps")
        fsc_ready, fhi_ready, fts = sem("fsc_ready"), sem("fhi_ready"), sem("fts")
        rows_ready, mean_pe, flag_ready = sem("rows_ready"), sem("mean_pe"), sem("flag_ready")
        g_in, g_x, g_rows = sem("g_in"), sem("g_x"), sem("g_rows")
        g_score, g_exp, g_tr, g_trc = sem("g_score"), sem("g_exp"), sem("g_tr"), sem("g_trc")
        g_pv, g_n, g_e, g_o, g_st = sem("g_pv"), sem("g_n"), sem("g_e"), sem("g_o"), sem("g_st")

        def is_fast(eng):
            eng.wait_ge(flag_ready, 1)
            return eng.value_load(flag[0:1, 0:1], min_val=0, max_val=1)

        def last_bank(r):
            return (None, bank[0], bank[1], bank[2], bank[3])[r][:, :].rearrange("p (n c) -> p n c", c=P)

        def last_end(r, ap):
            return ap[:, 2 * r - 2:2 * r, :, :].rearrange("p t k c -> p (t k) c")

        block = ctx.enter_context(nc.Block())

        @block.sync
        def _(sp):
            sp.dma_start(xa[:, 0:XT, :], x_t[:, 0:XT, :]).then_inc(x_in[0], 16)
            sp.wait_ge(w_zero, 1)
            for h in range(HALVES):
                sp.dma_start(w2[h * F:(h + 1) * F, h * FX:h * FX + F], w).then_inc(w_in, 16)
            for k in range(2):
                sp.dma_start(a2[:, k:k + 1], a[k * F:(k + 1) * F, :]).then_inc(w_in, 16)
            for g in range(1, XG):
                sp.dma_start(xa[:, bass.ts(g, XT), :], x_t[:, bass.ts(g, XT), :]).then_inc(x_in[g], 16)

            def load(b, c, slot):
                sp.dma_start(slots[:, slot], adj_t[:, bass.ds(b * RT, RT), bass.ds(c * JC, JC)])\
                    .then_inc(adj_in[slot], 16)

            for k in range(SLOTS - 1):
                load(0, k, k)
            sp.wait_ge(sdT_ready, 1)
            sp.dma_start(sd_dram.rearrange("k (t p) -> (k t) p", p=P), sdT[:, :]).then_inc(sd_out, 16)
            sp.wait_ge(sd_out, 16)
            sp.dma_start(s_rows[:, 0:IB], sd_dram[0:1, 0:IB].to_broadcast([P, IB])).then_inc(rows_in, 16)
            load(0, SLOTS - 1, SLOTS - 1)
            fast = is_fast(sp)
            with sp.If(fast == 1):
                def turn(b, m, used):
                    for k in range(SLOTS):
                        sp.wait_ge(adj_used, used + (k + 1) * SPL)
                        load(b, m * SLOTS + k, k)

                TURNS = NS // CYC
                with sp.Fori(0, TURNS - 1) as m:
                    turn(0, m + 1, m * CYC)
                with sp.Fori(0, NB - 1) as b:
                    sp.dma_start(s_rows[:, bass.ds(b * IB + IB, IB)],
                                 sd_dram[0:1, bass.ds(b * IB + IB, IB)].to_broadcast([P, IB]))\
                        .then_inc(rows_in, 16)
                    with sp.Fori(0, TURNS) as m:
                        turn(b + 1, m, b * NS + m * CYC + (NS - CYC))
                rows = (NB - 1) * RT
                sp.wait_ge(res_done, NB - 1)
                sp.dma_start(res, x_t[:, rows:rows + RT, :]).then_inc(last_x, 16)
                for h in range(2):
                    sp.wait_ge(last_rows, h + 1)
                    sp.dma_start(out_t[:, rows + h * RT // 2:rows + (h + 1) * RT // 2, :],
                                 num[:, bass.ts(h, RT // 2), :]).then_inc(last_out, 16)
                sp.wait_ge(last_out, 32)
            with sp.If(fast == 0):
                for k in range(SLOTS):
                    sp.wait_ge(adj_in[k], 16)
                sp.wait_ge(adj_used, LEAD)
                sp.wait_ge(rows_in, 16)
                sp.dma_start(d_rows[:, :], sd_dram[1:2, :].to_broadcast([P, N])).then_inc(g_rows, 16)
                with sp.Fori(0, T) as t:
                    sp.wait_ge(g_score, t + 1)
                    sp.dma_start(gen_adj, adj[bass.ds(t * P, P), :]).then_inc(g_in, 16)
                    sp.wait_ge(g_o, t + 1)
                    sp.dma_start(gen_x, x[bass.ds(t * P, P), :]).then_inc(g_x, 16)

        @block.gpsimd
        def _(pool):
            def held():
                pool.sem_inc(pool_waits, 1)

            nc.gpsimd.memset(w2[:, :], 0.0).then_inc(w_zero, 1)
            nc.gpsimd.memset(ident[:, :], 0.0).then_inc(pool_s, 1)
            nc.gpsimd.memset(ones_n[:, :], 1.0 / N).then_inc(pool_s, 1)
            nc.gpsimd.memset(den_pad[:, :, :, :, :], 0.0).then_inc(pool_s, 1)
            pool.wait_ge(pool_s, 3)

            def put(ap, value, base, pattern):
                return nc.gpsimd.affine_select(out=ap, in_=ap, compare_op=ALU.not_equal, fill=value,
                                               base=base, pattern=pattern, channel_multiplier=1)

            put(ident[:, :], 1.0, 0, [[-1, P]]).then_inc(pool_s, 1)
            pool.wait_ge(pool_s, 4)
            nc.gpsimd.tensor_copy(ident16[:, :], ident[:, :]).then_inc(consts, 1)
            for g in range(XG // 2, XG):
                tiles = bass.ts(g, XT)
                pool.wait_ge(x_mean, g - XG // 2 + 1)
                nc.gpsimd.tensor_tensor(xa[:, tiles, :], xa[:, tiles, :],
                                        stat[:, 0, tiles].unsqueeze(2).to_broadcast([P, XT, F]),
                                        ALU.subtract).then_inc(centered, 1)
            pool.wait_ge(ext_ready, 1)
            nc.gpsimd.partition_all_reduce(allx[:, 0:2], ext[:, 0:2], P, MAX).then_inc(ext_all, 1)
            nc.gpsimd.partition_all_reduce(allx[:, 2:3], ext[:, 2:3], P, ADD).then_inc(ext_all, 1)
            fast = is_fast(pool)
            with pool.If(fast == 1):
                pool.wait_ge(scaled_ready, 2)
                nc.gpsimd.tensor_tensor(fscaled[1], wh[:, 0:XT, :],
                                        scaled[:, 1, 0:XT].unsqueeze(2).to_broadcast([P, XT, F]),
                                        ALU.mult).then_inc(fsc1_ready, 1)
                pool.wait_ge(den_w_ready, 2)

                def pads(b, m):
                    for buf in range(2):
                        pool.wait_ge(masks_free, b * NS + m * 2 + buf + 1)
                        held()
                        nc.gpsimd.tensor_copy(den_pad[:, buf, :, :, 0:2],
                                              den_w[:, :, bass.ds((m * 2 + buf) * JT, JT), :])\
                            .then_inc(pad_ready, 1)

                def block_end(b, part):
                    links = 17

                    def tie(ins, k):
                        ins.then_inc(pool_c, 1)
                        pool.wait_ge(pool_c, b * links + k)
                        held()

                    def row_factors(pattern, **sizes):
                        return row_f[:, bass.ds(b * RT, RT), :].rearrange(pattern, **sizes)

                    def wide(ap):
                        return ap.unsqueeze(2).to_broadcast([P, RT, F])

                    if part == 0:
                        pool.dma_start(res, x_t[:, bass.ds(b * RT, RT), :]).then_inc(res_in, 16)
                        pool.wait_ge(round_act, b * RND + 2)
                        held()
                        tie(nc.gpsimd.tensor_scalar(den_end[:, :, :, :, 1], den_end[:, :, :, :, 1],
                                                    1.0 / LO, 0.0, ALU.mult, ALU.add), 1)
                        tie(nc.gpsimd.tensor_tensor(den_k[:, :, :, :], den_end[:, :, :, :, 0],
                                                    den_end[:, :, :, :, 1], ALU.add), 2)
                        for k in range(2):
                            ins = nc.gpsimd.tensor_tensor(
                                den_k[:, :, k, :], den_k[:, :, k, :],
                                row_factors("p (h t) k -> p t h k", h=2)[:, :, :, k], ALU.mult)
                            tie(ins, 3 + k)
                        tie(nc.gpsimd.tensor_tensor(
                            den_row[:, :, :].rearrange("p h t -> p t h"),
                            den_k[:, :, 0, :], den_k[:, :, 1, :], ALU.add), 5)
                        tie(nc.gpsimd.tensor_scalar(no_edge[:, :, :], den_row[:, :, :], 0.0, None,
                                                    ALU.is_equal), 6)
                        ins = nc.gpsimd.tensor_tensor(den_row[:, :, :], den_row[:, :, :],
                                                      no_edge[:, :, :], ALU.add)
                        ins.then_inc(den_ready, 1)
                    if part == 1:
                        pool.wait_ge(round_act, (b + 1) * RND + 1)
                        held()
                        tie(nc.gpsimd.tensor_scalar(end_lo, end_lo, 1.0 / LO, 0.0,
                                                    ALU.mult, ALU.add), 7)
                        tie(nc.gpsimd.tensor_tensor(end_lo, end_lo, ends[:, :, :, 0:F], ALU.add), 8)
                    if part == 2:
                        for k in range(2):
                            tie(nc.gpsimd.tensor_tensor(end_lo[:, :, k, :], end_lo[:, :, k, :],
                                                        wide(row_factors("p t k -> p t k")[:, :, k]),
                                                        ALU.mult), 9 + k)
                        nc.gpsimd.tensor_tensor(num, end_lo[:, :, 0, :], end_lo[:, :, 1, :], ALU.add)\
                            .then_inc(pool_c, 1)
                        pool.wait_ge(pool_c, b * links + 11)
                        pool.sem_inc(ends_free, 1)
                    if part == 3:
                        pool.wait_ge(recip_ready, b + 1)
                        held()
                        tie(nc.gpsimd.tensor_scalar(recip[:, :], recip[:, :], sc[:, 5:6], DTOP / VTOP,
                                                    ALU.mult, ALU.mult), 12)
                        tie(nc.gpsimd.tensor_tensor(num, num, wide(recip[:, :]), ALU.mult), 13)
                        tie(nc.gpsimd.tensor_tensor(
                            elu, mean_wh[:, :].unsqueeze(1).to_broadcast([P, RT, F]),
                            wide(no_edge[:, :, :].rearrange("p h t -> p (h t)")), ALU.mult), 14)
                        tie(nc.gpsimd.tensor_tensor(num, num, elu, ALU.add), 15)
                        nc.gpsimd.tensor_scalar(elu, num, 0.0, None, ALU.min).then_inc(elu_in, 1)
                    if part == 4:
                        pool.wait_ge(elu_out, b + 1)
                        held()
                        tie(nc.gpsimd.tensor_scalar(num, num, 0.0, -1.0, ALU.max, ALU.add), 16)
                        pool.wait_ge(res_in, b * 16 + 16)
                        held()
                        tie(nc.gpsimd.tensor_tensor(elu, elu, res, ALU.add), 17)
                        nc.gpsimd.tensor_tensor(num, num, elu, ALU.add).then_inc(res_done, 1)
                        pool.wait_ge(res_done, b + 1)
                        held()
                        pool.dma_start(out_t[:, bass.ds(b * RT, RT), :], num).then_inc(stored, 16)
                    if part == 5:
                        pool.wait_ge(stored, b * 16 + 16)
                        held()

                pool.sem_inc(ends_free, 1)
                END_PAIRS = (JOIN, JOIN + 1, JOIN + 2, EXP_STEP // 2 + 1, NP - 1)
                def features(n, part):
                    k, tiles = n % 2, bass.ts(1 + n // 2, XT)
                    if part == 0:
                        nc.gpsimd.tensor_tensor(fscaled[0], wh[:, tiles, :],
                                                scaled[:, k, tiles].unsqueeze(2).to_broadcast([P, XT, F]),
                                                ALU.mult).then_inc(fsc_ready, 1)
                    else:
                        pool.wait_ge(fhi_ready, 3 + n)
                        nc.gpsimd.tensor_scalar(fscaled[1], feats[:, k, tiles, 0:F], -LO, 0.0, ALU.mult, ALU.add)\
                            .then_inc(feat_c, 1)
                        pool.wait_ge(feat_c, 2 * n + 1)
                        nc.gpsimd.tensor_tensor(feats[:, k, tiles, F:P], fscaled[1], fscaled[0], ALU.add)\
                            .then_inc(feat_c, 1)
                        pool.wait_ge(feat_c, 2 * n + 2)
                        pool.sem_inc(fts, 1)

                pads(0, 0)
                pool.wait_ge(fts, 2)
                features(0, 0)
                pool.wait_ge(sums8_in, 1)
                n = 8
                while n > 1:
                    n //= 2
                    nc.gpsimd.tensor_tensor(sums8[:, 0:n, :] if n > 1 else mean_wh[:, :].unsqueeze(1),
                                            sums8[:, 0:n, :], sums8[:, n:2 * n, :], ALU.add)\
                        .then_inc(mean_in, 1)
                    pool.wait_ge(mean_in, 3 - n.bit_length() + 1)
                for m in range(NP):
                    if m:
                        pads(0, m)
                    for n, at_step in enumerate(VALUE_STEPS):
                        if m == at_step // 2:
                            features(n, 1)
                            if n + 1 < ITEMS:
                                features(n + 1, 0)
                with pool.Fori(0, NB - 1) as b:
                    for m in range(NP):
                        pads(b + 1, m)
                        if m == 1:
                            block_end(b, 0)
                        elif m in END_PAIRS:
                            block_end(b, 1 + END_PAIRS.index(m))
            with pool.If(fast == 0):
                pool.sem_inc(gen_free, 1)
                with pool.Fori(0, T) as t:
                    pool.wait_ge(g_o, t + 2)
                    held()
                    pool.dma_start(out[bass.ds(t * P, P), :], gen_o).then_inc(g_st, 16)
                    pool.wait_ge(g_st, t * 16 + 16)
                    pool.sem_inc(gen_free, 1)

        @block.scalar
        def _(act):
            def convert(slot, part, turn_no, step):
                act.wait_ge(adj_in[slot], turn_no * 16 + 16)
                if step is not None:
                    act.wait_ge(mask_used, (step + 1) * JT)
                nc.scalar.activation(mask[:, part % 2], slots[:, slot, :, bass.ts(part, JP)],
                                     ACT.Sign, bias=minus_half).then_inc(adj_used, 1)

            for g in range(XG):
                tiles = bass.ts(g, XT)
                act.wait_ge(centered, g + 1)
                nc.scalar.activation(sq[:, tiles, :], xa[:, tiles, :], ACT.Square).then_inc(sq_done, 1)
                for n in range(XQ // 4):
                    act.wait_ge(xT_done, g * (XQ // 4) + n + 1)
                    nc.scalar.activation(hT[:, bass.ts(g * (XQ // 4) + n, 512)],
                                         bank[(g * (XQ // 4) + n) % 2][:, :], ACT.Relu)\
                        .then_inc(relu_done, 1)
                if g >= XG - LEAD:
                    step = g - (XG - LEAD)
                    convert(step // SPL, step % SPL, 0, None)
                act.wait_ge(var_ready, g + 1)
                nc.scalar.activation(stat[:, 2, tiles], stat[:, 1, tiles], ACT.Sqrt).then_inc(root_done, 1)
            act.wait_ge(sdT_pe, 1)
            nc.scalar.activation(sdT[:, :], end[:, 0:P], ACT.Copy).then_inc(sdT_ready, 1)
            act.wait_ge(scal, 1)
            nc.scalar.activation(e_pos[:, :], sd[:, 1, :], ACT.Exp, bias=sc[:, 0:1]).then_inc(exps, 1)
            nc.scalar.activation(e_neg[:, :], sd[:, 1, :], ACT.Exp, bias=sc[:, 1:2], scale=ALPHA)\
                .then_inc(exps, 1)
            act.wait_ge(rows_ready, 1)
            nc.scalar.activation(row_f[:, :, 0], stat[:, 4, :], ACT.Exp, scale=1 - ALPHA)\
                .then_inc(exps, 1)
            nc.scalar.activation(row_f[:, :, 1], stat[:, 5, :], ACT.Exp, scale=ALPHA - 1)\
                .then_inc(exps, 1)
            fast = is_fast(act)
            with act.If(fast == 1):
                for k, ready in enumerate((fsc_ready, fsc1_ready)):
                    act.wait_ge(ready, 1)
                    nc.scalar.activation(feats[:, k, 0:XT, 0:F], fscaled[k], ACT.Copy, scale=1 / LO)\
                        .then_inc(fhi_ready, 1)
                act.wait_ge(mean_pe, 1)
                nc.scalar.activation(sums8.rearrange("p n f -> p (n f)"), end[:, :], ACT.Copy).then_inc(sums8_in, 1)

                def value_part(n):
                    act.wait_ge(fsc_ready, 2 + n)
                    nc.scalar.activation(feats[:, n % 2, bass.ts(1 + n // 2, XT), 0:F], fscaled[0],
                                         ACT.Copy, scale=1 / LO).then_inc(fhi_ready, 1)

                def negatives(g, buf, n):
                    act.wait_ge(coded, (g + 1) * JT)
                    act.wait_ge(masks_free, g + 1)
                    nc.scalar.activation(m_neg[:, buf, 0:n], code[:, buf, 0:n], ACT.Relu, scale=-1.0)\
                        .then_inc(neg_act, 1)

                def copy_sums(b):
                    act.wait_ge(round_pe, b * RND + 1)
                    for h in range(2):
                        act.wait_ge(sums_done, b * 4 + 2 * h + 1)
                        nc.scalar.activation(acc_sb[:, 0, bass.ts(h, 512)], acc[0][h][:, :], ACT.Copy)\
                            .then_inc(acc_act, 1)

                def copy_den(b):
                    act.wait_ge(masks_free, (b + 1) * NS + 2)
                    nc.scalar.activation(den_sb, den[:, :], ACT.Copy).then_inc(acc_act, 1)

                def copy_round(b, r):
                    act.wait_ge(round_pe, b * RND + r + 2)
                    if r == 0:
                        act.wait_ge(ends_free, b + 1)
                        rows = end[:, :].rearrange("p (t g c) -> p (t g) c", t=4, g=4)[:, :, 0:2]
                        nc.scalar.activation(den_end[:, :, :, :, :].rearrange("p t k h c -> p (t k h) c"),
                                             rows, ACT.Copy).then_inc(round_act, 1)
                    else:
                        nc.scalar.activation(ends[:, 2 * r - 2:2 * r, :, :].rearrange("p t k c -> p (t k c)"),
                                             end[:, :], ACT.Copy).then_inc(round_act, 1)

                def exp_end(b):
                    act.wait_ge(elu_in, b + 1)
                    nc.scalar.activation(elu, elu, ACT.Exp).then_inc(elu_out, 1)

                TURNS = NS // CYC

                def turn(b, m, ended=None, last=False, items=False, exp=False):
                    for r in range(CYC):
                        g = b * NS + m * CYC + r
                        if not (last and r + LEAD >= CYC):
                            rr = (r + LEAD) % CYC
                            convert(rr // SPL, rr % SPL, b * TURNS + m + (r + LEAD) // CYC, g)
                        if items and m * CYC + r in VALUE_STEPS:
                            value_part(VALUE_STEPS.index(m * CYC + r))
                        if ended is not None:
                            if m == 0 and r == 0:
                                copy_sums(ended)
                            if m * CYC + r in COPIES:
                                copy_round(ended, COPIES.index(m * CYC + r))
                        light = (ended is not None and m * CYC + r in LIGHT or items and m * CYC + r in VALUE_STEPS
                                 or exp and r == 0)
                        negatives(g, r % 2, WA_END if light else WA)
                        if ended is not None and m == 0 and r == 0:
                            copy_den(ended)

                turn(0, 0, items=True)
                turn(0, 1, items=True)
                turn(0, 2, items=True)
                with act.Fori(3, TURNS) as m:
                    turn(0, m)
                with act.Fori(0, NB - 2) as b:
                    for m in range(END_TURNS):
                        turn(b + 1, m, ended=b)
                    with act.Fori(END_TURNS, TURNS - 1) as m:
                        turn(b + 1, m)
                    exp_end(b)
                    turn(b + 1, TURNS - 1, exp=True)
                for m in range(END_TURNS):
                    turn(NB - 1, m, ended=NB - 2)
                with act.Fori(END_TURNS, TURNS - 1) as m:
                    turn(NB - 1, m)
                exp_end(NB - 2)
                turn(NB - 1, TURNS - 1, last=True, exp=True)
                copy_sums(NB - 1)
                copy_den(NB - 1)
                act.wait_ge(ends_free, NB)
                for r in range(RND):
                    act.wait_ge(last_pe, r + 1)
                    if r == 0:
                        rows = end[:, :].rearrange("p (t g c) -> p (t g) c", t=4, g=4)[:, :, 0:2]
                        nc.scalar.activation(den_end[:, :, :, :, :].rearrange("p t k h c -> p (t k h) c"),
                                             rows, ACT.Copy).then_inc(last_den, 1)
                    else:
                        nc.scalar.activation(last_end(r, end_lo), last_bank(r)[:, :, F:P], ACT.Copy,
                                             scale=1 / LO).then_inc(last_low, 1)
                for h in range(2):
                    act.wait_ge(last_min, h + 1)
                    half = elu[:, bass.ts(h, RT // 2), :]
                    nc.scalar.activation(half, half, ACT.Exp).then_inc(last_exp, 1)
            with act.If(fast == 0):
                with act.Fori(0, T) as t:
                    act.wait_ge(g_score, t + 2)
                    nc.scalar.activation(gen_p, gen_p, ACT.Exp, bias=g1[:, 1:2], accum_out=g1[:, 2:3])\
                        .then_inc(g_exp, 1)
                    act.wait_ge(g_n, t + 1)
                    nc.scalar.activation(gen_e, gen_e, ACT.Exp).then_inc(g_e, 1)

        @block.vector
        def _(v):
            chain = [0]

            def link(ins):
                chain[0] += 1
                ins.then_inc(dve, 1)
                v.wait_ge(dve, chain[0])

            def over_f(ap):
                return ap.unsqueeze(2).to_broadcast([*ap.shape, F])

            nc.vector.memset(minus_half, -0.5).then_inc(consts, 1)
            v.wait_ge(wT_done, 1)
            nc.vector.tensor_copy(wT[:, 0:F], end[0:F, 0:F]).then_inc(wTc, 1)
            nc.vector.tensor_copy(wT[:, F:P], end[0:F, 0:F]).then_inc(wTc, 1)
            link(nc.vector.tensor_tensor(w_sq, w2[:, :], w2[:, :], ALU.mult))
            link(nc.vector.tensor_reduce(ext[:, 2:3], w_sq, AX.X, ALU.add))

            def centre(g):
                tiles = bass.ts(g, XT)
                v.wait_ge(x_in[g], 16)
                link(nc.vector.tensor_reduce(stat[:, 0, tiles], xa[:, tiles, :], AX.X, ALU.add))
                mean = nc.vector.tensor_scalar(stat[:, 0, tiles], stat[:, 0, tiles], 1.0 / F, None, ALU.mult)
                if g >= XG // 2:
                    mean.then_inc(x_mean, 1)
                    return
                link(mean)
                nc.vector.tensor_tensor(xa[:, tiles, :], xa[:, tiles, :], over_f(stat[:, 0, tiles]),
                                        ALU.subtract).then_inc(centered, 1)

            def root(g):
                tiles = bass.ts(g, XT)
                v.wait_ge(sq_done, g + 1)
                link(nc.vector.tensor_reduce(stat[:, 0, tiles], sq[:, tiles, :], AX.X, ALU.add))
                nc.vector.tensor_scalar(stat[:, 1, tiles], stat[:, 0, tiles], 1.0 / F, EPS,
                                        ALU.mult, ALU.add).then_inc(var_ready, 1)
                v.wait_ge(var_ready, g + 1)
                v.wait_ge(root_done, g + 1)
                link(nc.vector.reciprocal(stat[:, 3, tiles], stat[:, 2, tiles]))
                link(nc.vector.tensor_tensor(stat[:, 4, tiles], stat[:, 3, tiles], stat[:, 3, tiles],
                                             ALU.mult))
                link(nc.vector.tensor_tensor(stat[:, 4, tiles], stat[:, 4, tiles], stat[:, 1, tiles],
                                             ALU.mult))
                link(nc.vector.tensor_scalar(stat[:, 4, tiles], stat[:, 4, tiles], -0.5, 1.5,
                                             ALU.mult, ALU.add))
                link(nc.vector.tensor_tensor(rstd[:, tiles], stat[:, 3, tiles], stat[:, 4, tiles],
                                             ALU.mult))

            def take(g):
                for n in range(g * (XT // 4), (g + 1) * (XT // 4)):
                    v.wait_ge(wh_pe, n + 1)
                    tiles = bass.ts(n, 4)
                    nc.vector.tensor_tensor(
                        whx[:, tiles, :], bank[2 + n % 4][:, 0:4 * FX].rearrange("p (t c) -> p t c", t=4),
                        rstd[:, tiles].unsqueeze(2).to_broadcast([P, 4, FX]), ALU.mult)\
                        .then_inc(wh_copied, 1)

            centre(0)
            v.wait_ge(wa_done, 1)
            for h in range(HALVES):
                hp = slice(h * F, (h + 1) * F)
                nc.vector.tensor_copy(w2[hp, h * FX + F:(h + 1) * FX], bank[6][hp, 0:2]).then_inc(wac, 1)
            centre(1)
            for g in range(XG):
                root(g)
                if g + 2 < XG:
                    centre(g + 2)
                take(g)
            v.wait_ge(wh_copied, T // 4)
            nc.vector.tensor_copy(sd[:, :, :], whx[:, :, F:FX].rearrange("p t k -> p k t"))\
                .then_inc(sd_ready, 1)
            link(nc.vector.tensor_reduce(ext[:, 0:1], whx[:, :, F + 1], AX.X, ALU.max))
            v.wait_ge(sd_ready, 1)
            link(nc.vector.tensor_scalar(neg_d[:, :], sd[:, 1, :], -1.0, None, ALU.mult))
            nc.vector.tensor_reduce(ext[:, 1:2], neg_d[:, :], AX.X, ALU.max).then_inc(ext_ready, 1)
            v.wait_ge(ext_all, 2)
            nc.vector.tensor_scalar(sc[:, 1:2], allx[:, 0:1], -ALPHA, None, ALU.mult)
            nc.vector.tensor_scalar(sc[:, 0:1], allx[:, 0:1], -1.0, None, ALU.mult).then_inc(scal, 1)
            link(nc.vector.tensor_tensor(sc[:, 2:3], allx[:, 0:1], allx[:, 1:2], ALU.add))
            link(nc.vector.tensor_scalar(sc[:, 3:4], sc[:, 2:3], SPAN, None, ALU.is_le))
            link(nc.vector.tensor_scalar(sc[:, 4:5], allx[:, 2:3], 1e-20, None, ALU.is_ge))
            link(nc.vector.tensor_tensor(sc[:, 3:4], sc[:, 3:4], sc[:, 4:5], ALU.mult))
            link(nc.vector.tensor_scalar(sc[:, 4:5], allx[:, 2:3], 1e20, None, ALU.is_le))
            nc.vector.tensor_tensor(flag[:, :], sc[:, 3:4], sc[:, 4:5], ALU.mult).then_inc(flag_ready, 1)
            link(nc.vector.tensor_scalar(sc[:, 5:6], allx[:, 2:3], 0.25 * float(F) ** 0.5,
                                         0.5 * float(F) ** 0.5, ALU.mult, ALU.add))
            link(nc.vector.reciprocal(sc[:, 6:7], sc[:, 5:6]))
            nc.vector.tensor_scalar(stat[:, 4, :], sd[:, 0, :], allx[:, 0:1], 0.0, ALU.add, ALU.min)
            nc.vector.tensor_scalar(stat[:, 5, :], sd[:, 0, :], allx[:, 0:1], 0.0,
                                    ALU.add, ALU.max).then_inc(rows_ready, 1)
            chained = chain[0]
            fast = is_fast(v)
            with v.If(fast == 1):
                for k, e in enumerate((e_pos, e_neg)):
                    v.wait_ge(exps, k + 1)
                    nc.vector.tensor_scalar(scaled[:, k, :], e[:, :], sc[:, 6:7], VTOP * LO,
                                            ALU.mult, ALU.mult).then_inc(scaled_ready, 1)
                v.wait_ge(scaled_ready, 1)
                nc.vector.tensor_tensor(fscaled[0], wh[:, 0:XT, :], over_f(scaled[:, 0, 0:XT]),
                                        ALU.mult).then_inc(fsc_ready, 1)
                for k, e in enumerate((e_pos, e_neg)):
                    link(nc.vector.tensor_scalar(den_w[:, k, :, 0], e[:, :], DTOP, None, ALU.mult))
                    link(nc.vector.tensor_scalar(stat[:, k, :], e[:, :], DTOP * LO, None, ALU.mult))
                    nc.vector.scalar_tensor_tensor(den_w[:, k, :, 1], den_w[:, k, :, 0], -LO,
                                                   stat[:, k, :], ALU.mult, ALU.add)\
                        .then_inc(den_w_ready, 1)
                for k, ready in enumerate((fsc_ready, fsc1_ready)):
                    v.wait_ge(fhi_ready, k + 1)
                    v.wait_ge(ready, 1)
                    nc.vector.scalar_tensor_tensor(feats[:, k, 0:XT, F:P], feats[:, k, 0:XT, 0:F], -LO,
                                                   fscaled[k], ALU.mult, ALU.add).then_inc(fts, 1)
                v.wait_ge(exps, 4)
                v.wait_ge(rows_in, 16)

                def encode(b, sj, buf, u, early):
                    g = b * NS + sj
                    if u == 0:
                        v.wait_ge(neg_act, g + 1)
                        if not early:
                            v.wait_ge(masks_dve, g - 1)
                    v.wait_ge(mask_used, g * JT + u + 1)
                    nc.vector.scalar_tensor_tensor(
                        code[:, buf, bass.ts(u, IB)], s_rows[:, bass.ds(b * IB, IB)],
                        neg_d[:, bass.ds(sj * JT + u, 1)], tr[u][:, :], ALU.is_gt, ALU.subtract)\
                        .then_inc(coded, 1)

                def masks(g, buf, n=WA):
                    v.wait_ge(masks_free, g + 1)
                    v.wait_ge(coded, (g + 1) * JT)
                    nc.vector.tensor_scalar(m_pos[:, buf, :], code[:, buf, :], 0.0, None, ALU.is_equal)
                    nc.vector.tensor_scalar(m_neg[:, buf, n:W], code[:, buf, n:W], -1.0, None,
                                            ALU.is_equal).then_inc(masks_dve, 1)

                def copy_sums(b, part):
                    v.wait_ge(sums_done, b * 4 + 2 * part + 2)
                    if part == 0:
                        v.wait_ge(round_pe, b * RND + 1)
                    nc.vector.tensor_copy(acc_sb[:, 1, bass.ts(part, 512)], acc[1][part][:, :])\
                        .then_inc(acc_dve, 1)

                def reciprocals(b):
                    v.wait_ge(den_ready, b + 1)
                    nc.vector.reciprocal(recip[:, :], den_row[:, :, :].rearrange("p h t -> p (h t)"))\
                        .then_inc(recip_ready, 1)

                def step(b, sj, buf, ended=None, light=False, first=False, early=False):
                    g = b * NS + sj
                    encode(b, sj, buf, 0, early)
                    if not first:
                        masks(g - 1, 1 - buf, WA_END if light else WA)
                    if ended is not None:
                        copy_sums(ended, 0)
                        copy_sums(ended, 1)
                    encode(b, sj, buf, 1, early)

                step(0, 0, 0, first=True, early=True)
                step(0, 1, 1, early=True)
                VS, VSTEP = VALUE_STEPS.start, VALUE_STEPS.step
                for sj in range(2, VSTEP):
                    step(0, sj, sj % 2, light=(sj - 1 == VS))
                with v.Fori(1, ITEMS) as m:
                    for r in range(VSTEP):
                        step(0, m * VSTEP + r, r % 2, light=(r - 1 == VS))
                with v.Fori(ITEMS * VSTEP // 2, NP) as m:
                    step(0, m * 2, 0)
                    step(0, m * 2 + 1, 1)
                with v.Fori(0, NB - 1) as b:
                    v.wait_ge(rows_in, b * 16 + 32)
                    step(b + 1, 0, 0)
                    for sj in range(1, END_TURNS * CYC):
                        step(b + 1, sj, sj % 2, light=(sj - 1 in LIGHT), ended=b if sj == 1 else None)
                    reciprocals(b)
                    with v.Fori(END_TURNS * CYC // 2, EXP_STEP // 2) as m:
                        step(b + 1, m * 2, 0)
                        step(b + 1, m * 2 + 1, 1)
                    for sj in (EXP_STEP, EXP_STEP + 1):
                        step(b + 1, sj, sj % 2, light=(sj - 1 == EXP_STEP))
                    with v.Fori(EXP_STEP // 2 + 1, NP) as m:
                        step(b + 1, m * 2, 0)
                        step(b + 1, m * 2 + 1, 1)
                masks(NB * NS - 1, 1)
                for part in range(2):
                    copy_sums(NB - 1, part)

                last_f = row_f[:, (NB - 1) * RT:, :]
                v.wait_ge(stored, (NB - 1) * 16)
                v.wait_ge(last_x, 16)
                link(nc.vector.tensor_scalar(res, res, -1.0, None, ALU.add))
                v.wait_ge(last_den, 1)
                link(nc.vector.scalar_tensor_tensor(den_k[:, :, :, :], den_end[:, :, :, :, 1], 1 / LO,
                                                    den_end[:, :, :, :, 0], ALU.mult, ALU.add))
                link(nc.vector.tensor_tensor(
                    den_k[:, :, :, :], den_k[:, :, :, :],
                    last_f.rearrange("p (h t) k -> p t k h", h=2), ALU.mult))
                link(nc.vector.tensor_tensor(den_row[:, :, :].rearrange("p h t -> p t h"),
                                             den_k[:, :, 0, :], den_k[:, :, 1, :], ALU.add))
                link(nc.vector.tensor_scalar(no_edge[:, :, :], den_row[:, :, :], 0.0, None, ALU.is_equal))
                link(nc.vector.tensor_tensor(den_row[:, :, :], den_row[:, :, :], no_edge[:, :, :], ALU.add))
                link(nc.vector.reciprocal(recip[:, :], den_row[:, :, :].rearrange("p h t -> p (h t)")))
                link(nc.vector.tensor_scalar(recip[:, :], recip[:, :], sc[:, 5:6], DTOP / VTOP,
                                             ALU.mult, ALU.mult))
                link(nc.vector.tensor_tensor(factors[:, :, :], last_f,
                                             recip[:, :].unsqueeze(2).to_broadcast([P, RT, 2]), ALU.mult))
                edges = no_edge[:, :, :].rearrange("p h t -> p (h t)")
                link(nc.vector.tensor_tensor(
                    elu, mean_wh[:, :].unsqueeze(1).to_broadcast([P, RT, F]), over_f(edges), ALU.mult))
                for h in range(2):
                    half = bass.ts(h, RT // 2)
                    for r in (2 * h + 1, 2 * h + 2):
                        v.wait_ge(last_pe, r + 1)
                        v.wait_ge(last_low, r)
                        lows = last_end(r, end_lo)
                        link(nc.vector.tensor_tensor(lows, lows, last_bank(r)[:, :, 0:F], ALU.add))
                    link(nc.vector.tensor_tensor(
                        end_lo[:, half, :, :], end_lo[:, half, :, :],
                        factors[:, half, :].unsqueeze(3).to_broadcast([P, RT // 2, 2, F]), ALU.mult))
                    link(nc.vector.tensor_tensor(num[:, half, :], end_lo[:, half, 0, :],
                                                 end_lo[:, half, 1, :], ALU.add))
                    link(nc.vector.tensor_tensor(num[:, half, :], num[:, half, :], elu[:, half, :], ALU.add))
                    nc.vector.tensor_scalar(elu[:, half, :], num[:, half, :], 0.0, None, ALU.min)\
                        .then_inc(last_min, 1)
                    link(nc.vector.scalar_tensor_tensor(num[:, half, :], num[:, half, :], 0.0,
                                                        res[:, half, :], ALU.max, ALU.add))
                for h in range(2):
                    half = bass.ts(h, RT // 2)
                    v.wait_ge(last_exp, h + 1)
                    nc.vector.tensor_tensor(num[:, half, :], num[:, half, :], elu[:, half, :], ALU.add)\
                        .then_inc(last_rows, 1)
            with v.If(fast == 0):
                v.wait_ge(mean_pe, 1)
                v.wait_ge(g_rows, 16)
                v.sem_inc(g_score, 1)
                v.sem_inc(g_o, 1)
                v.sem_inc(g_trc, 1)
                GCH = 12
                with v.Fori(0, T) as t:
                    def tie(ins, k):
                        ins.then_inc(dve, 1)
                        v.wait_ge(dve, chained + t * GCH + k)

                    v.wait_ge(g_in, t * 16 + 16)
                    v.wait_ge(g_pv, t + 1)
                    tie(nc.vector.tensor_scalar(gen_p, gen_adj, 0.0, OFF, ALU.is_le, ALU.mult), 1)
                    tie(nc.vector.tensor_tensor(gen_p, gen_p, d_rows[:, :], ALU.add), 2)
                    tie(nc.vector.tensor_reduce(g1[:, 0:1], gen_p, AX.X, ALU.max), 3)
                    s_col = sd[:, 0, bass.ds(t, 1)]
                    tie(nc.vector.tensor_scalar(gen_p, gen_p, s_col, None, ALU.add), 4)
                    tie(nc.vector.tensor_scalar(g1[:, 0:1], g1[:, 0:1], s_col, None, ALU.add), 5)
                    tie(nc.vector.scalar_tensor_tensor(g1[:, 3:4], g1[:, 0:1], ALPHA, g1[:, 0:1],
                                                       ALU.mult, ALU.max), 6)
                    tie(nc.vector.tensor_scalar(g1[:, 1:2], g1[:, 3:4], -1.0, None, ALU.mult), 7)
                    nc.vector.scalar_tensor_tensor(gen_p, gen_p, ALPHA, gen_p, ALU.mult, ALU.max)\
                        .then_inc(g_score, 1)
                    for c in range(T // 4):
                        v.wait_ge(g_tr, t * (T // 4) + c + 1)
                        nc.vector.tensor_copy(gen_pT[:, bass.ts(c % 2, 512)], bank[c % 2][:, :])\
                            .then_inc(g_trc, 1)
                    v.wait_ge(g_pv, t + 2)
                    v.wait_ge(g_exp, t + 1)
                    tie(nc.vector.reciprocal(g1[:, 4:5], g1[:, 2:3]), 8)
                    v.wait_ge(gen_free, t + 1)
                    tie(nc.vector.tensor_scalar(gen_o, bank[2][:, 0:F], g1[:, 4:5], None, ALU.mult), 9)
                    nc.vector.tensor_scalar(gen_e, gen_o, 0.0, None, ALU.min).then_inc(g_n, 1)
                    v.wait_ge(g_x, t * 16 + 16)
                    tie(nc.vector.scalar_tensor_tensor(gen_o, gen_o, 0.0, gen_x, ALU.max, ALU.add), 10)
                    v.wait_ge(g_e, t + 1)
                    tie(nc.vector.tensor_scalar(gen_e, gen_e, -1.0, None, ALU.add), 11)
                    tie(nc.vector.tensor_tensor(gen_o, gen_e, gen_o, ALU.add), 12)
                    nc.vector.tensor_copy(g1[:, 5:6], g1[:, 4:5]).then_inc(g_o, 1)

        @block.tensor
        def _(pe):
            def transposes(g, buf, u, first=False):
                if u == 0:
                    pe.wait_ge(adj_used, g + 1)
                if not first:
                    pe.wait_ge(coded, (g - 1) * JT + u + 1)
                for r in range(RT):
                    last = nc.tensor.transpose(tr[u][:, bass.ts(r, P)],
                                               mask[:, buf, r, bass.ts(u, P)], ident16[:, :])
                last.then_inc(mask_used, 1)

            pe.wait_ge(consts, 2)
            pe.wait_ge(w_in, 64)
            nc.tensor.transpose(end[0:F, 0:F], w2[0:F, 0:F], ident[0:F, 0:F]).then_inc(wT_done, 1)
            pe.wait_ge(wTc, 2)
            nc.tensor.matmul(bank[6][:, 0:2], wT[:, :], a2[:, :], start=True, stop=True)\
                .then_inc(wa_done, 1)

            def turn_x(g):
                pe.wait_ge(centered, g + 1)
                for n in range(g * (XQ // 4), (g + 1) * (XQ // 4)):
                    if n >= 2:
                        pe.wait_ge(relu_done, n - 1)
                    for u in range(4):
                        q = 4 * n + u
                        last = nc.tensor.transpose(bank[n % 2][:, bass.ts(u, P)],
                                                   xa[:, 2 * q:2 * q + 2, :].rearrange("p t f -> p (t f)"),
                                                   ident[:, :])
                    last.then_inc(xT_done, 1)

            turn_x(0)
            pe.wait_ge(wac, 2)
            for g in range(XG):
                if g + 1 < XG:
                    turn_x(g + 1)
                for n in range(g * (XQ // 2), (g + 1) * (XQ // 2)):
                    pe.wait_ge(relu_done, n // 2 + 1)
                    if n >= 4:
                        pe.wait_ge(wh_copied, n - 3)
                    for u in range(2):
                        last = nc.tensor.matmul(bank[2 + n % 4][:, bass.ts(u, HALVES * FX)],
                                                hT[:, bass.ts(2 * n + u, P)], w2[:, :],
                                                start=True, stop=True)
                    last.then_inc(wh_pe, 1)
            pe.wait_ge(sd_ready, 1)
            nc.tensor.transpose(end[:, 0:P], sd[:, :, :].rearrange("p k t -> p (k t)"), ident[:, :])\
                .then_inc(sdT_pe, 1)
            for u in range(JT):
                transposes(0, 0, u, first=True)
            for free in (neg_act, masks_free):
                nc.tensor.transpose(den[:, :].bitcast(fp16)[:, 0:P], ident16[:, :], ident16[:, :])\
                    .then_inc(free, 2)
            pe.wait_ge(sdT_ready, 1)
            pe.wait_ge(wh_copied, T // 4)
            for n in range(T // 8):
                last = nc.tensor.matmul(end[:, :], ones_n[:, :], wh[:, bass.ts(n, 8), :],
                                        start=(n == 0), stop=(n == T // 8 - 1))
            last.then_inc(mean_pe, 1)
            fast = is_fast(pe)
            with pe.If(fast == 1):
                def numerators(b, sj, buf, start, stop, ended):
                    g = b * NS + sj
                    pe.wait_ge(masks_dve, g + 1)
                    pe.wait_ge(neg_act, g + 3)
                    order = [(u, k, h) for u in range(JT) for k in range(2) for h in range(2)]
                    if start or stop:
                        order = [(u, k, h) for h in range(2) for k in range(2) for u in range(JT)]
                    for u, k, h in order:
                        if ended is not None and u == 0:
                            if k == 0:
                                pe.wait_ge(acc_act, 3 * ended + h + 1)
                            else:
                                pe.wait_ge(acc_dve, 2 * ended + h + 1)
                        last = nc.tensor.matmul(acc[k][h][:, :],
                                                feats[:, k, bass.ds(sj * JT + u, 1), :]
                                                .rearrange("p t c -> p (t c)"),
                                                (m_pos, m_neg)[k][:, buf, u * IB + h * 512:
                                                                  u * IB + (h + 1) * 512],
                                                start=start and u == 0, stop=stop and u == JT - 1)
                        if stop and u == JT - 1:
                            last.then_inc(sums_done, 1)

                def denominators(b, sj, buf, start, stop, ended):
                    g = b * NS + sj
                    if ended is not None:
                        pe.wait_ge(acc_act, 3 * ended + 3)
                    pe.wait_ge(pad_ready, g + 1)
                    for u in range(JT):
                        s0, s1 = start and u == 0, stop and u == JT - 1
                        for k, m in enumerate((m_pos, m_neg)):
                            for h in range(2):
                                p0 = (2 * k + h) * DW
                                last = nc.tensor.matmul(den[p0:p0 + DW, :], den_pad[:, buf, k, u, :],
                                                        m[:, buf, u * IB + h * 512:u * IB + (h + 1) * 512],
                                                        start=s0, stop=s1, tile_position=(0, p0))
                    last.then_inc(masks_free, 1)

                def end_round(b, r):
                    if r == 0:
                        pe.wait_ge(acc_act, 3 * b + 3)
                        pe.wait_ge(acc_dve, 2 * b + 2)
                    pe.wait_ge(round_act, b * RND + r + 1)
                    for n in range(4):
                        if r == 0:
                            src = den_sb[:, bass.ts(n, P)]
                        else:
                            src = acc_sb[:, n % 2, bass.ts(2 * (r - 1) + n // 2, P)]
                        last = nc.tensor.transpose(end[:, bass.ts(n, P)], src, ident[:, :])
                    last.then_inc(round_pe, 1)

                def step(b, sj, buf, start=False, stop=False, ended=None, ahead=True):
                    g = b * NS + sj
                    if ahead:
                        transposes(g + 2, buf, 0)
                    numerators(b, sj, buf, start, stop, ended)
                    if ahead:
                        transposes(g + 2, buf, 1)
                    denominators(b, sj, buf, start, stop, ended)

                for u in range(JT):
                    transposes(1, 1, u)
                pe.sem_inc(round_pe, 1)
                pe.sem_inc(round_act, 1)
                pe.wait_ge(fts, 2)
                step(0, 0, 0, start=True)
                step(0, 1, 1)
                for g in range(XG):
                    if g:
                        pe.wait_ge(fts, 2 * g + 2)
                    with pe.Fori(max(g * (NP // XG), 1), min((g + 1) * (NP // XG), NP - 1)) as m:
                        step(0, m * 2, 0)
                        step(0, m * 2 + 1, 1)
                step(0, NS - 2, 0)
                step(0, NS - 1, 1, stop=True)

                def block_steps(b, ended, ahead=True):
                    PEEL = (GAP * (RND - 1)) // 2 + 1
                    for sj in range(2 * PEEL):
                        step(b, sj, sj % 2, start=(sj == 0), ended=ended if sj == 0 else None)
                        if sj % GAP == 0 and sj // GAP < RND:
                            end_round(ended, sj // GAP)
                    with pe.Fori(PEEL, NP - 1) as m:
                        step(b, m * 2, 0)
                        step(b, m * 2 + 1, 1)
                    step(b, NS - 2, 0, ahead=ahead)
                    step(b, NS - 1, 1, stop=True, ahead=ahead)

                with pe.Fori(0, NB - 2) as b:
                    block_steps(b + 1, b)
                block_steps(NB - 1, NB - 2, ahead=False)
                pe.wait_ge(acc_act, 3 * NB)
                pe.wait_ge(acc_dve, 2 * NB)
                pe.wait_ge(round_act, (NB - 1) * RND + 1)
                for r in range(RND):
                    for n in range(4):
                        if r == 0:
                            last = nc.tensor.transpose(end[:, bass.ts(n, P)], den_sb[:, bass.ts(n, P)],
                                                       ident[:, :])
                        else:
                            last = nc.tensor.transpose(last_bank(r)[:, n, :],
                                                       acc_sb[:, n % 2, bass.ts(2 * (r - 1) + n // 2, P)],
                                                       ident[:, :])
                    last.then_inc(last_pe, 1)
            with pe.If(fast == 0):
                pe.sem_inc(g_pv, 1)
                with pe.Fori(0, T) as t:
                    pe.wait_ge(g_exp, t + 1)
                    pe.wait_ge(g_o, t + 1)

                    def turn_p(c):
                        pe.wait_ge(g_trc, t * (T // 4) + max(c - 2, 0) + (c > 1) + 1)
                        for u in range(4):
                            last = nc.tensor.transpose(bank[c % 2][:, bass.ts(u, P)],
                                                       gen_p[:, bass.ts(4 * c + u, P)], ident[:, :])
                        last.then_inc(g_tr, 1)

                    turn_p(0)
                    for c in range(T // 4):
                        if c + 1 < T // 4:
                            turn_p(c + 1)
                        pe.wait_ge(g_trc, t * (T // 4) + c + 2)
                        for u in range(4):
                            j = 4 * c + u
                            last = nc.tensor.matmul(bank[2][:, 0:F],
                                                    gen_pT[:, (c % 2) * 512 + u * P:(c % 2) * 512 + (u + 1) * P],
                                                    wh[:, j, :], start=(j == 0), stop=(j == T - 1))
                    last.then_inc(g_pv, 1)


_INS = ["x", "adj", "L0_gnn_W", "L0_gnn_a"]


def kernel(**inputs):
    import numpy as _np
    import concourse.bacc as _bacc
    from concourse import mybir as _mybir
    from concourse.bass_utils import run_bass_kernel_spmd as _run

    nc = _bacc.Bacc("TRN2", target_bir_lowering=False, num_devices=1)
    arrays, args = {}, []
    for name in _INS:
        arr = _np.ascontiguousarray(inputs[name])
        arrays[f"in_{name}"] = arr
        args.append(nc.dram_tensor(f"in_{name}", arr.shape, _mybir.dt.from_np(arr.dtype),
                                   kind="ExternalInput").ap())
    shape = arrays["in_x"].shape
    args.append(nc.dram_tensor("out_x", shape, _mybir.dt.float32, kind="ExternalOutput").ap())
    gat_preln_program(nc, *args)
    r = _run(nc, [arrays], core_ids=[0])
    return r.results[0]["out_x"]
```
